# Optimizing a Trainium2 kernel written in Bass

```python
import numpy as np
import jax
import jax.numpy as jnp

def _softmax(x, axis=-1):
    return jax.nn.softmax(x, axis=axis)

def _gelu(x):
    return jax.nn.gelu(x, approximate=True)

def _silu(x):
    return jax.nn.silu(x)

def _sigmoid(x):
    return jax.nn.sigmoid(x)

def _layernorm(x, axis=-1, eps=1e-05):
    m = jnp.mean(x, axis=axis, keepdims=True)
    v = jnp.var(x, axis=axis, keepdims=True)
    return (x - m) / jnp.sqrt(v + eps)

def _scatter_add(tgt, idx, src, axis=0):
    return tgt.at[idx].add(src)

def _segment_sum(src, seg, n):
    return jax.ops.segment_sum(src, seg, n)
kernel_name = 'mk_xattn_ffn_d4_seqx_r8_e3e9dd'

def setup_inputs(seed: int=0):
    np.random.seed(seed)
    _w = jnp.asarray

    def _rec_inputs():
        import jax
        import jax.numpy as jnp
        _rk = jax.random.key(seed)
        x = -0.0002928 + 1 * jax.random.normal(jax.random.fold_in(_rk, 1), (8, 256, 128), jnp.float32)
        _lenS = 256 - jax.random.randint(jax.random.fold_in(_rk, 7), (8,), 0, max(1, 256 // 4) + 1, jnp.int32)
        _lenS2 = 256 - jax.random.randint(jax.random.fold_in(_rk, 8), (8,), 0, max(1, 256 // 4) + 1, jnp.int32)
        _ctx_1024P = jax.random.normal(jax.random.fold_in(_rk, 11), (8, 16, 128), jnp.float32)
        _ctx_1024c = jax.random.dirichlet(jax.random.fold_in(_rk, 511), 0.3 * jnp.ones((16,), jnp.float32), (8, 256))
        _ctx_1024t = jnp.einsum('bsk,bkd->bsd', _ctx_1024c, _ctx_1024P)
        _ctx_1024t = _ctx_1024t * jax.lax.rsqrt(jnp.mean(jnp.square(_ctx_1024t)) + 1e-12) * 0.953939
        ctx_1024 = -1.39393e-06 + 0.999914 * (_ctx_1024t + 0.3 * jax.random.normal(jax.random.fold_in(_rk, 611), (8, 256, 128), jnp.float32))
        fside_1x1xSxS2_0 = 0.000376506 + 0.999991 * jax.random.normal(jax.random.fold_in(_rk, 13), (1, 1, 256, 256), jnp.float32)
        _validS = jnp.arange(256)[None, :] < _lenS[:, None]
        _validS2 = jnp.arange(256)[None, :] < _lenS2[:, None]
        _causal = jnp.tril(jnp.ones((256, 256), dtype=bool))
        mask_1x1xSxS2_ik0 = jnp.where(jnp.broadcast_to(_validS2[0:1, None, None, :], (1, 1, 256, 256)), 0, 1).astype(jnp.int32)
        mask_1x1xSxS2_fk0 = jnp.where(jnp.broadcast_to(_validS2[0:1, None, None, :], (1, 1, 256, 256)), -1000000000.0, 0.0).astype(jnp.float32)
        mask_1x1xSxS2_ik1 = jnp.where(jnp.broadcast_to(_validS2[0:1, None, None, :], (1, 1, 256, 256)), 1, 0).astype(jnp.int32)
        return (x, ctx_1024, fside_1x1xSxS2_0, mask_1x1xSxS2_ik0, mask_1x1xSxS2_fk0, mask_1x1xSxS2_ik1)
    x, ctx_1024, fside_1x1xSxS2_0, mask_1x1xSxS2_ik0, mask_1x1xSxS2_fk0, mask_1x1xSxS2_ik1 = _rec_inputs()

    def _L0_xattn_setup():
        import math
        import jax, jax.numpy as jnp
        import numpy as np
        N_HEAD = 16

        def _slopes(n_head):
            cp2 = 2 ** int(math.floor(math.log2(n_head)))
            slopes = 0.5 ** np.arange(1, cp2 + 1)
            if cp2 < n_head:
                intra = 1.0 / math.sqrt(2.0)
                pair = intra ** np.arange(1, 1 + 2 * (n_head - cp2), 2)
                slopes = np.sort(np.concatenate([slopes, pair]))[::-1]
            return jnp.asarray(slopes, dtype=jnp.float32)

        def _alibi_bias(S):
            d = jnp.arange(S)[:, None] - jnp.arange(S)[None, :]
            return -jnp.maximum(d, 0).astype(jnp.float32)
        key = jax.random.key(seed)
        B, S, D = (2, 256, 128)
        ks = jax.random.split(key, 12)
        f = lambda k, sh: jax.random.normal(k, sh, dtype=jnp.float32)
        inp = {'q': f(ks[0], (B, S, D)), 'k': f(ks[1], (B, S, D)), 'v': f(ks[2], (B, S, D)), 'mask': jnp.tril(jnp.ones((S, S), dtype=jnp.int32))[None, None], 'wq_w': f(ks[3], (D, D)) * 0.02, 'wq_b': f(ks[4], (D,)) * 0.02, 'wk_w': f(ks[5], (D, D)) * 0.02, 'wk_b': f(ks[6], (D,)) * 0.02, 'wv_w': f(ks[7], (D, D)) * 0.02, 'wv_b': f(ks[8], (D,)) * 0.02, 'out_w': f(ks[9], (D, D)) * 0.02, 'out_b': f(ks[10], (D,)) * 0.02}
        return inp
    _L0_xattn_all = _L0_xattn_setup()
    _L0_xattn_in = {k: v for k, v in _L0_xattn_all.items() if k in ('wq_w', 'wq_b', 'wk_w', 'wk_b', 'wv_w', 'wv_b', 'out_w', 'out_b')}
    del _L0_xattn_all

    def _L0_ffn_setup():
        import jax, jax.numpy as jnp
        import numpy as np
        B, S, D = (4, 512, 128)
        E, I = (8, 256)
        CAPACITY = 2
        K = max(1, int(S / E * CAPACITY))
        key = jax.random.key(seed)
        k1, k2, k3, k4, k5 = jax.random.split(key, 5)
        x = jax.random.normal(k1, (B, S, D), dtype=jnp.float32)
        gate_w = jax.random.normal(k2, (D, E), dtype=jnp.float32) * 0.006
        Wg = jax.random.normal(k3, (E, D, I), dtype=jnp.float32) * 0.02
        Wu = jax.random.normal(k4, (E, D, I), dtype=jnp.float32) * 0.02
        Wd = jax.random.normal(k5, (E, I, D), dtype=jnp.float32) * 0.02
        return {'x': x, 'gate_w': gate_w, 'Wg': Wg, 'Wu': Wu, 'Wd': Wd}
    _L0_ffn_all = _L0_ffn_setup()
    _L0_ffn_in = {k: v for k, v in _L0_ffn_all.items() if k in ('gate_w', 'Wg', 'Wu', 'Wd')}
    del _L0_ffn_all

    def _L1_xattn_setup():
        import jax, jax.numpy as jnp
        import numpy as np
        HIDDEN = 128
        HEADS = 16
        DEPTH = HIDDEN // HEADS
        B, F, T = (2, 256, 256)
        key = jax.random.key(seed)
        ks = jax.random.split(key, 7)
        return {'query_input': jax.random.normal(ks[0], (B, F, HIDDEN), dtype=jnp.float32), 'source_input': jax.random.normal(ks[1], (B, T, HIDDEN), dtype=jnp.float32), 'bias': jax.random.normal(ks[2], (1, 1, F, T), dtype=jnp.float32), 'wq': jax.random.normal(ks[3], (HIDDEN, HEADS, DEPTH), dtype=jnp.float32) * 0.02, 'wk': jax.random.normal(ks[4], (HIDDEN, HEADS, DEPTH), dtype=jnp.float32) * 0.02, 'wv': jax.random.normal(ks[5], (HIDDEN, HEADS, DEPTH), dtype=jnp.float32) * 0.02, 'wo': jax.random.normal(ks[6], (HEADS, DEPTH, HIDDEN), dtype=jnp.float32) * 0.02}
    _L1_xattn_all = _L1_xattn_setup()
    _L1_xattn_in = {k: v for k, v in _L1_xattn_all.items() if k in ('wq', 'wk', 'wv', 'wo')}
    del _L1_xattn_all

    def _L1_ffn_setup():
        import jax, jax.numpy as jnp
        import numpy as np
        B, T, C = (2, 256, 128)
        H, D = (16, 64)
        CR = 8
        R = C // CR
        ROPE = D // 2
        NOPE = D - ROPE
        E, K, I, S = (8, 2, 64, 1)
        THETA = 100000.0
        EPS = 1e-05

        def _rmsnorm(x, w):
            rms = jnp.sqrt(jnp.mean(x * x, axis=-1, keepdims=True) + EPS)
            return w * (x / rms)

        def _rope(xh):
            d = xh.shape[-1]
            t = jnp.arange(xh.shape[2], dtype=jnp.float32)
            freqs = 1.0 / THETA ** (jnp.arange(0, d, 2, dtype=jnp.float32) / d)
            ang = jnp.outer(t, freqs)
            cos, sin = (jnp.cos(ang), jnp.sin(ang))
            xr = xh.reshape(xh.shape[:-1] + (d // 2, 2))
            x0, x1 = (xr[..., 0], xr[..., 1])
            rot = jnp.stack([x0 * cos - x1 * sin, x0 * sin + x1 * cos], axis=-1)
            return rot.reshape(xh.shape)

        def _attention(x, Wq, Wkva, Wkvb, Wo):
            b, t, _ = x.shape
            q = (x @ Wq).reshape(b, t, H, D).transpose(0, 2, 1, 3)
            ckv = x @ Wkva
            kv_latent, k_rope = (ckv[:, :, :R], ckv[:, :, R:])
            kv = (kv_latent @ Wkvb).reshape(b, t, H, NOPE).transpose(0, 2, 1, 3)
            k_rope = jnp.broadcast_to(k_rope[:, None, :, :], (b, H, t, ROPE))
            q_nope, q_rope = (q[..., :NOPE], q[..., NOPE:])
            q = jnp.concatenate([q_nope, _rope(q_rope)], axis=-1)
            k = jnp.concatenate([kv, _rope(k_rope)], axis=-1)
            v = jnp.concatenate([kv, jnp.zeros_like(k_rope)], axis=-1)
            att = jnp.einsum('bhqd,bhkd->bhqk', q, k) / jnp.sqrt(jnp.float32(D))
            mask = jnp.tril(jnp.ones((t, t), dtype=bool))
            att = jnp.where(mask, att, jnp.float32(-jnp.inf))
            att = jax.nn.softmax(att, axis=-1)
            y = jnp.einsum('bhqk,bhkd->bhqd', att, v)
            y = y.transpose(0, 2, 1, 3).reshape(b, t, H * D)
            return y @ Wo

        def _experts(x_flat, Wg, Wu, Wd):
            g = jax.nn.silu(jnp.einsum('nc,eci->nei', x_flat, Wg))
            u = jnp.einsum('nc,eci->nei', x_flat, Wu)
            return jnp.einsum('nei,eic->nec', g * u, Wd)

        def _moe(x, Wgate, expert_bias, Wg, Wu, Wd, sWg, sWu, sWd):
            b, t, c = x.shape
            xf = x.reshape(-1, c)
            shared = jnp.mean(_experts(xf, sWg, sWu, sWd), axis=1)
            logits = xf @ Wgate + expert_bias
            probs = jax.nn.softmax(logits, axis=-1)
            topk_p, topk_i = jax.lax.top_k(probs, K)
            topk_p = topk_p / jnp.sum(topk_p, axis=-1, keepdims=True)
            comb = jnp.sum(jax.nn.one_hot(topk_i, E, dtype=xf.dtype) * topk_p[..., None], axis=1)
            routed = jnp.einsum('ne,nec->nc', comb, _experts(xf, Wg, Wu, Wd))
            return (shared + routed).reshape(b, t, c)
        key = jax.random.key(seed)
        ks = jax.random.split(key, 16)
        w = lambda k, shp: jax.random.normal(k, shp, dtype=jnp.float32) * 0.02
        return {'x': jax.random.normal(ks[0], (B, T, C), dtype=jnp.float32), 'w_ln1': jnp.ones((C,), jnp.float32), 'Wq': w(ks[1], (C, H * D)), 'Wkva': w(ks[2], (C, R + ROPE)), 'Wkvb': w(ks[3], (R, H * NOPE)), 'Wo': w(ks[4], (H * D, C)), 'w_ln2': jnp.ones((C,), jnp.float32), 'Wgate': w(ks[5], (C, E)), 'expert_bias': jnp.zeros((E,), jnp.float32), 'Wg': w(ks[6], (E, C, I)), 'Wu': w(ks[7], (E, C, I)), 'Wd': w(ks[8], (E, I, C)), 'sWg': w(ks[9], (S, C, I)), 'sWu': w(ks[10], (S, C, I)), 'sWd': w(ks[11], (S, I, C))}
    _L1_ffn_all = _L1_ffn_setup()
    _L1_ffn_in = {k: v for k, v in _L1_ffn_all.items() if k in ('w_ln1', 'Wq', 'Wkva', 'Wkvb', 'Wo', 'w_ln2', 'Wgate', 'expert_bias', 'Wg', 'Wu', 'Wd', 'sWg', 'sWu', 'sWd')}
    del _L1_ffn_all

    def _L2_xattn_setup():
        import jax, jax.numpy as jnp
        import numpy as np
        H = 16
        D_MODEL = 128
        B, S = (2, 256)
        DH = D_MODEL // H
        key = jax.random.key(seed)
        ks = jax.random.split(key, 12)
        std = 0.02
        q = jax.random.normal(ks[0], (B, S, D_MODEL), dtype=jnp.float32)
        k = jax.random.normal(ks[1], (B, S, D_MODEL), dtype=jnp.float32)
        v = jax.random.normal(ks[2], (B, S, D_MODEL), dtype=jnp.float32)
        causal = jnp.tril(jnp.ones((S, S), dtype=bool))
        mask = jnp.where(causal, 0.0, -1000000000.0).astype(jnp.float32)[None, None, :, :]

        def dense(kk):
            return (jax.random.normal(kk, (D_MODEL, D_MODEL), dtype=jnp.float32) * std, jnp.zeros((D_MODEL,), dtype=jnp.float32))
        Wq, bq = dense(ks[3])
        Wk, bk = dense(ks[4])
        Wv, bv = dense(ks[5])
        Wo, bo = dense(ks[6])
        return {'q': q, 'k': k, 'v': v, 'mask': mask, 'Wq': Wq, 'bq': bq, 'Wk': Wk, 'bk': bk, 'Wv': Wv, 'bv': bv, 'Wo': Wo, 'bo': bo}
    _L2_xattn_all = _L2_xattn_setup()
    _L2_xattn_in = {k: v for k, v in _L2_xattn_all.items() if k in ('Wq', 'bq', 'Wk', 'bk', 'Wv', 'bv', 'Wo', 'bo')}
    del _L2_xattn_all

    def _L2_ffn_setup():
        import jax, jax.numpy as jnp
        import numpy as np
        B, N, D, F, E, K = (4, 256, 128, 512, 16, 2)
        EPS = 1e-05
        key = jax.random.key(seed)
        ks = jax.random.split(key, 6)
        scaled = lambda k, shape, fan: jax.random.normal(k, shape, jnp.float32) / np.float32(np.sqrt(fan))
        return {'x': jax.random.normal(ks[0], (B, N, D), jnp.float32), 'Wr': scaled(ks[1], (D, E), D), 'br': jnp.zeros((E,), jnp.float32), 'W1': scaled(ks[2], (E, D, F), D), 'W3': scaled(ks[3], (E, D, F), D), 'W2': scaled(ks[4], (E, F, D), F), 'gamma': jnp.ones((E, D), jnp.float32), 'beta': jnp.zeros((E, D), jnp.float32)}
    _L2_ffn_all = _L2_ffn_setup()
    _L2_ffn_in = {k: v for k, v in _L2_ffn_all.items() if k in ('Wr', 'br', 'W1', 'W3', 'W2', 'gamma', 'beta')}
    del _L2_ffn_all

    def _L3_xattn_setup():
        import jax, jax.numpy as jnp
        import numpy as np
        D_MODEL = 128
        H = 16
        D_K = D_MODEL // H
        key = jax.random.key(seed)
        ks = jax.random.split(key, 12)
        B, S = (2, 256)
        inp = {'q': jax.random.normal(ks[0], (B, S, D_MODEL), jnp.float32), 'k': jax.random.normal(ks[1], (B, S, D_MODEL), jnp.float32), 'v': jax.random.normal(ks[2], (B, S, D_MODEL), jnp.float32), 'mask': jax.random.randint(ks[3], (1, 1, S, S), 0, 2, jnp.int32)}
        s = 1.0 / np.sqrt(D_MODEL)
        inp['wq_w'] = jax.random.normal(ks[4], (D_MODEL, D_MODEL), jnp.float32) * s
        inp['wq_b'] = jnp.zeros((D_MODEL,), jnp.float32)
        inp['wk_w'] = jax.random.normal(ks[5], (D_MODEL, D_MODEL), jnp.float32) * s
        inp['wk_b'] = jnp.zeros((D_MODEL,), jnp.float32)
        inp['wv_w'] = jax.random.normal(ks[6], (D_MODEL, D_MODEL), jnp.float32) * s
        inp['wv_b'] = jnp.zeros((D_MODEL,), jnp.float32)
        inp['wo_w'] = jax.random.normal(ks[7], (D_MODEL, D_MODEL), jnp.float32) * s
        inp['wo_b'] = jnp.zeros((D_MODEL,), jnp.float32)
        return inp
    _L3_xattn_all = _L3_xattn_setup()
    _L3_xattn_in = {k: v for k, v in _L3_xattn_all.items() if k in ('wq_w', 'wq_b', 'wk_w', 'wk_b', 'wv_w', 'wv_b', 'wo_w', 'wo_b')}
    del _L3_xattn_all

    def _L3_ffn_setup():
        import jax, jax.numpy as jnp
        import numpy as np
        BLOCK = 32
        W_BITS = 4
        ACT_BITS = 16

        def act_qdq(x):
            qmax = 2.0 ** (ACT_BITS - 1) - 1.0
            scale = jnp.maximum(jnp.max(jnp.abs(x)) / qmax, 1e-12)
            return jnp.clip(jnp.round(x / scale), -qmax - 1.0, qmax) * scale

        def fixed_qdq_u16(x):
            scale = 1.0 / 65536.0
            return jnp.clip(jnp.round(x / scale), 0.0, 65535.0) * scale

        def lpbq_dequant(w):
            O, I = w.shape
            qmax = 2.0 ** (W_BITS - 1) - 1.0
            wb = w.reshape(O, I // BLOCK, BLOCK)
            s = jnp.maximum(jnp.max(jnp.abs(wb), axis=-1, keepdims=True) / qmax, 1e-12)
            wq = jnp.clip(jnp.round(wb / s), -qmax - 1.0, qmax) * s
            return wq.reshape(O, I)
        key = jax.random.key(seed)
        k1, k2, k3, k4 = jax.random.split(key, 4)
        B, S, H, I = (2, 512, 128, 384)
        x = jax.random.normal(k1, (B, S, H), jnp.float32)
        w_gate = jax.random.normal(k2, (I, H), jnp.float32) * 0.02
        w_up = jax.random.normal(k3, (I, H), jnp.float32) * 0.02
        w_down = jax.random.normal(k4, (H, I), jnp.float32) * 0.02
        return {'x': x, 'w_gate': w_gate, 'w_up': w_up, 'w_down': w_down}
    _L3_ffn_all = _L3_ffn_setup()
    _L3_ffn_in = {k: v for k, v in _L3_ffn_all.items() if k in ('w_gate', 'w_up', 'w_down')}
    del _L3_ffn_all
    return {'x': x, 'ctx_1024': ctx_1024, 'fside_1x1xSxS2_0': fside_1x1xSxS2_0, 'mask_1x1xSxS2_ik0': mask_1x1xSxS2_ik0, 'mask_1x1xSxS2_fk0': mask_1x1xSxS2_fk0, 'mask_1x1xSxS2_ik1': mask_1x1xSxS2_ik1, 'L0_xattn_wq_w': _L0_xattn_in['wq_w'], 'L0_xattn_wq_b': _L0_xattn_in['wq_b'], 'L0_xattn_wk_w': _L0_xattn_in['wk_w'], 'L0_xattn_wk_b': _L0_xattn_in['wk_b'], 'L0_xattn_wv_w': _L0_xattn_in['wv_w'], 'L0_xattn_wv_b': _L0_xattn_in['wv_b'], 'L0_xattn_out_w': _L0_xattn_in['out_w'], 'L0_xattn_out_b': _L0_xattn_in['out_b'], 'L0_ffn_gate_w': _L0_ffn_in['gate_w'], 'L0_ffn_Wg': _L0_ffn_in['Wg'], 'L0_ffn_Wu': _L0_ffn_in['Wu'], 'L0_ffn_Wd': _L0_ffn_in['Wd'], 'L1_xattn_wq': _L1_xattn_in['wq'], 'L1_xattn_wk': _L1_xattn_in['wk'], 'L1_xattn_wv': _L1_xattn_in['wv'], 'L1_xattn_wo': _L1_xattn_in['wo'], 'L1_ffn_w_ln1': _L1_ffn_in['w_ln1'], 'L1_ffn_Wq': _L1_ffn_in['Wq'], 'L1_ffn_Wkva': _L1_ffn_in['Wkva'], 'L1_ffn_Wkvb': _L1_ffn_in['Wkvb'], 'L1_ffn_Wo': _L1_ffn_in['Wo'], 'L1_ffn_w_ln2': _L1_ffn_in['w_ln2'], 'L1_ffn_Wgate': _L1_ffn_in['Wgate'], 'L1_ffn_expert_bias': _L1_ffn_in['expert_bias'], 'L1_ffn_Wg': _L1_ffn_in['Wg'], 'L1_ffn_Wu': _L1_ffn_in['Wu'], 'L1_ffn_Wd': _L1_ffn_in['Wd'], 'L1_ffn_sWg': _L1_ffn_in['sWg'], 'L1_ffn_sWu': _L1_ffn_in['sWu'], 'L1_ffn_sWd': _L1_ffn_in['sWd'], 'L2_xattn_Wq': _L2_xattn_in['Wq'], 'L2_xattn_bq': _L2_xattn_in['bq'], 'L2_xattn_Wk': _L2_xattn_in['Wk'], 'L2_xattn_bk': _L2_xattn_in['bk'], 'L2_xattn_Wv': _L2_xattn_in['Wv'], 'L2_xattn_bv': _L2_xattn_in['bv'], 'L2_xattn_Wo': _L2_xattn_in['Wo'], 'L2_xattn_bo': _L2_xattn_in['bo'], 'L2_ffn_Wr': _L2_ffn_in['Wr'], 'L2_ffn_br': _L2_ffn_in['br'], 'L2_ffn_W1': _L2_ffn_in['W1'], 'L2_ffn_W3': _L2_ffn_in['W3'], 'L2_ffn_W2': _L2_ffn_in['W2'], 'L2_ffn_gamma': _L2_ffn_in['gamma'], 'L2_ffn_beta': _L2_ffn_in['beta'], 'L3_xattn_wq_w': _L3_xattn_in['wq_w'], 'L3_xattn_wq_b': _L3_xattn_in['wq_b'], 'L3_xattn_wk_w': _L3_xattn_in['wk_w'], 'L3_xattn_wk_b': _L3_xattn_in['wk_b'], 'L3_xattn_wv_w': _L3_xattn_in['wv_w'], 'L3_xattn_wv_b': _L3_xattn_in['wv_b'], 'L3_xattn_wo_w': _L3_xattn_in['wo_w'], 'L3_xattn_wo_b': _L3_xattn_in['wo_b'], 'L3_ffn_w_gate': _L3_ffn_in['w_gate'], 'L3_ffn_w_up': _L3_ffn_in['w_up'], 'L3_ffn_w_down': _L3_ffn_in['w_down']}

def reference(x, ctx_1024, fside_1x1xSxS2_0, mask_1x1xSxS2_ik0, mask_1x1xSxS2_fk0, mask_1x1xSxS2_ik1, L0_xattn_wq_w, L0_xattn_wq_b, L0_xattn_wk_w, L0_xattn_wk_b, L0_xattn_wv_w, L0_xattn_wv_b, L0_xattn_out_w, L0_xattn_out_b, L0_ffn_gate_w, L0_ffn_Wg, L0_ffn_Wu, L0_ffn_Wd, L1_xattn_wq, L1_xattn_wk, L1_xattn_wv, L1_xattn_wo, L1_ffn_w_ln1, L1_ffn_Wq, L1_ffn_Wkva, L1_ffn_Wkvb, L1_ffn_Wo, L1_ffn_w_ln2, L1_ffn_Wgate, L1_ffn_expert_bias, L1_ffn_Wg, L1_ffn_Wu, L1_ffn_Wd, L1_ffn_sWg, L1_ffn_sWu, L1_ffn_sWd, L2_xattn_Wq, L2_xattn_bq, L2_xattn_Wk, L2_xattn_bk, L2_xattn_Wv, L2_xattn_bv, L2_xattn_Wo, L2_xattn_bo, L2_ffn_Wr, L2_ffn_br, L2_ffn_W1, L2_ffn_W3, L2_ffn_W2, L2_ffn_gamma, L2_ffn_beta, L3_xattn_wq_w, L3_xattn_wq_b, L3_xattn_wk_w, L3_xattn_wk_b, L3_xattn_wv_w, L3_xattn_wv_b, L3_xattn_wo_w, L3_xattn_wo_b, L3_ffn_w_gate, L3_ffn_w_up, L3_ffn_w_down):
    import jax
    import jax.numpy as jnp

    def _L0_xattn_ref(q, k, v, mask, wq_w, wq_b, wk_w, wk_b, wv_w, wv_b, out_w, out_b):
        import math
        import jax, jax.numpy as jnp
        import numpy as np
        N_HEAD = 16

        def _slopes(n_head):
            cp2 = 2 ** int(math.floor(math.log2(n_head)))
            slopes = 0.5 ** np.arange(1, cp2 + 1)
            if cp2 < n_head:
                intra = 1.0 / math.sqrt(2.0)
                pair = intra ** np.arange(1, 1 + 2 * (n_head - cp2), 2)
                slopes = np.sort(np.concatenate([slopes, pair]))[::-1]
            return jnp.asarray(slopes, dtype=jnp.float32)

        def _alibi_bias(S):
            d = jnp.arange(S)[:, None] - jnp.arange(S)[None, :]
            return -jnp.maximum(d, 0).astype(jnp.float32)
        B, S, D = q.shape
        H = N_HEAD
        hd = D // H
        lin = lambda x, w, b: x @ w.T + b
        split = lambda x: x.reshape(B, S, H, hd).transpose(0, 2, 1, 3)
        wq = split(lin(q, wq_w, wq_b))
        wk = split(lin(k, wk_w, wk_b))
        wv = split(lin(v, wv_w, wv_b))
        qk = jnp.einsum('bhsd,bhtd->bhst', wq, wk)
        alibi = _alibi_bias(S)[None, :, :] * _slopes(H)[:, None, None]
        attn = qk + alibi[None]
        attn = jnp.where(mask == 0, jnp.float32(-1000000000.0), attn)
        attn = jax.nn.softmax(attn, axis=-1)
        out = jnp.einsum('bhst,bhtd->bhsd', attn, wv)
        out = out.transpose(0, 2, 1, 3).reshape(B, S, D)
        return lin(out, out_w, out_b)

    def _L0_ffn_ref(x, gate_w, Wg, Wu, Wd):
        import jax, jax.numpy as jnp
        import numpy as np
        B, S, D = (4, 512, 128)
        E, I = (8, 256)
        CAPACITY = 2
        K = max(1, int(S / E * CAPACITY))
        logits = jnp.einsum('bsd,de->bse', x, gate_w)
        affinity = jax.nn.softmax(logits, axis=-1)
        affinity_T = jnp.transpose(affinity, (0, 2, 1))
        gating, index = jax.lax.top_k(affinity_T, K)
        b_idx = jnp.arange(x.shape[0])[:, None, None]
        x_sel = x[b_idx, index]
        g = jnp.einsum('bekd,edi->beki', x_sel, Wg)
        u = jnp.einsum('bekd,edi->beki', x_sel, Wu)
        h = jax.nn.silu(g) * u
        out = jnp.einsum('beki,eid->bekd', h, Wd)
        contrib = out * gating[..., None]
        x_out = jnp.zeros_like(x).at[b_idx, index].add(contrib)
        return x_out

    def _L1_xattn_ref(query_input, source_input, bias, wq, wk, wv, wo):
        import jax, jax.numpy as jnp
        import numpy as np
        HIDDEN = 128
        HEADS = 16
        DEPTH = HIDDEN // HEADS
        B, F, T = (2, 256, 256)
        q = jnp.einsum('bfc,cnh->bfnh', query_input, wq)
        k = jnp.einsum('btc,cnh->btnh', source_input, wk)
        v = jnp.einsum('btc,cnh->btnh', source_input, wv)
        q = q * DEPTH ** (-0.5)
        logits = jnp.einsum('btnh,bfnh->bnft', k, q)
        logits = logits + bias
        weights = jax.nn.softmax(logits, axis=3)
        attn = jnp.einsum('bnft,btnh->bfnh', weights, v)
        out = jnp.einsum('bfnh,nhe->bfe', attn, wo)
        return out

    def _L1_ffn_ref(x, w_ln1, Wq, Wkva, Wkvb, Wo, w_ln2, Wgate, expert_bias, Wg, Wu, Wd, sWg, sWu, sWd):
        import jax, jax.numpy as jnp
        import numpy as np
        B, T, C = (2, 256, 128)
        H, D = (16, 64)
        CR = 8
        R = C // CR
        ROPE = D // 2
        NOPE = D - ROPE
        E, K, I, S = (8, 2, 64, 1)
        THETA = 100000.0
        EPS = 1e-05

        def _rmsnorm(x, w):
            rms = jnp.sqrt(jnp.mean(x * x, axis=-1, keepdims=True) + EPS)
            return w * (x / rms)

        def _rope(xh):
            d = xh.shape[-1]
            t = jnp.arange(xh.shape[2], dtype=jnp.float32)
            freqs = 1.0 / THETA ** (jnp.arange(0, d, 2, dtype=jnp.float32) / d)
            ang = jnp.outer(t, freqs)
            cos, sin = (jnp.cos(ang), jnp.sin(ang))
            xr = xh.reshape(xh.shape[:-1] + (d // 2, 2))
            x0, x1 = (xr[..., 0], xr[..., 1])
            rot = jnp.stack([x0 * cos - x1 * sin, x0 * sin + x1 * cos], axis=-1)
            return rot.reshape(xh.shape)

        def _attention(x, Wq, Wkva, Wkvb, Wo):
            b, t, _ = x.shape
            q = (x @ Wq).reshape(b, t, H, D).transpose(0, 2, 1, 3)
            ckv = x @ Wkva
            kv_latent, k_rope = (ckv[:, :, :R], ckv[:, :, R:])
            kv = (kv_latent @ Wkvb).reshape(b, t, H, NOPE).transpose(0, 2, 1, 3)
            k_rope = jnp.broadcast_to(k_rope[:, None, :, :], (b, H, t, ROPE))
            q_nope, q_rope = (q[..., :NOPE], q[..., NOPE:])
            q = jnp.concatenate([q_nope, _rope(q_rope)], axis=-1)
            k = jnp.concatenate([kv, _rope(k_rope)], axis=-1)
            v = jnp.concatenate([kv, jnp.zeros_like(k_rope)], axis=-1)
            att = jnp.einsum('bhqd,bhkd->bhqk', q, k) / jnp.sqrt(jnp.float32(D))
            mask = jnp.tril(jnp.ones((t, t), dtype=bool))
            att = jnp.where(mask, att, jnp.float32(-jnp.inf))
            att = jax.nn.softmax(att, axis=-1)
            y = jnp.einsum('bhqk,bhkd->bhqd', att, v)
            y = y.transpose(0, 2, 1, 3).reshape(b, t, H * D)
            return y @ Wo

        def _experts(x_flat, Wg, Wu, Wd):
            g = jax.nn.silu(jnp.einsum('nc,eci->nei', x_flat, Wg))
            u = jnp.einsum('nc,eci->nei', x_flat, Wu)
            return jnp.einsum('nei,eic->nec', g * u, Wd)

        def _moe(x, Wgate, expert_bias, Wg, Wu, Wd, sWg, sWu, sWd):
            b, t, c = x.shape
            xf = x.reshape(-1, c)
            shared = jnp.mean(_experts(xf, sWg, sWu, sWd), axis=1)
            logits = xf @ Wgate + expert_bias
            probs = jax.nn.softmax(logits, axis=-1)
            topk_p, topk_i = jax.lax.top_k(probs, K)
            topk_p = topk_p / jnp.sum(topk_p, axis=-1, keepdims=True)
            comb = jnp.sum(jax.nn.one_hot(topk_i, E, dtype=xf.dtype) * topk_p[..., None], axis=1)
            routed = jnp.einsum('ne,nec->nc', comb, _experts(xf, Wg, Wu, Wd))
            return (shared + routed).reshape(b, t, c)
        x = x + _attention(_rmsnorm(x, w_ln1), Wq, Wkva, Wkvb, Wo)
        residual = x
        xn = _rmsnorm(x, w_ln2)
        x_out = _moe(xn, Wgate, expert_bias, Wg, Wu, Wd, sWg, sWu, sWd)
        return residual + x_out

    def _L2_xattn_ref(q, k, v, mask, Wq, bq, Wk, bk, Wv, bv, Wo, bo):
        import jax, jax.numpy as jnp
        import numpy as np
        H = 16
        D_MODEL = 128
        B, S = (2, 256)
        DH = D_MODEL // H
        b, s, d = q.shape

        def split_heads(x):
            return x.reshape(b, s, H, DH).transpose(0, 2, 1, 3)
        qh = split_heads(q @ Wq + bq)
        kh = split_heads(k @ Wk + bk)
        vh = split_heads(v @ Wv + bv)
        scale = 1.0 / jnp.sqrt(jnp.asarray(DH, dtype=qh.dtype))
        scores = jnp.einsum('bhqd,bhkd->bhqk', qh, kh) * scale + mask
        weights = jax.nn.softmax(scores, axis=-1)
        ctx = jnp.einsum('bhqk,bhkd->bhqd', weights, vh)
        ctx = ctx.transpose(0, 2, 1, 3).reshape(b, s, d)
        return ctx @ Wo + bo

    def _L2_ffn_ref(x, Wr, br, W1, W3, W2, gamma, beta):
        import jax, jax.numpy as jnp
        import numpy as np
        B, N, D, F, E, K = (4, 256, 128, 512, 16, 2)
        EPS = 1e-05
        b, n, d = x.shape
        e = Wr.shape[1]
        xf = x.reshape(-1, d)
        logits = xf @ Wr + br
        probs = jax.nn.softmax(logits, axis=-1)
        vals, idx = jax.lax.top_k(probs, K)
        w = vals / vals.sum(axis=-1, keepdims=True)
        combine = jnp.zeros((xf.shape[0], e), x.dtype)
        for k in range(K):
            combine = combine + w[:, k:k + 1] * jax.nn.one_hot(idx[:, k], e, dtype=x.dtype)
        out = jnp.zeros_like(xf)
        for ei in range(e):
            h = jax.nn.silu(xf @ W1[ei]) * (xf @ W3[ei])
            y = h @ W2[ei]
            mu = y.mean(axis=-1, keepdims=True)
            var = ((y - mu) ** 2).mean(axis=-1, keepdims=True)
            y = (y - mu) * jax.lax.rsqrt(var + EPS) * gamma[ei] + beta[ei]
            out = out + combine[:, ei:ei + 1] * y
        return out.reshape(b, n, d)

    def _L3_xattn_ref(q, k, v, mask, wq_w, wq_b, wk_w, wk_b, wv_w, wv_b, wo_w, wo_b):
        import jax, jax.numpy as jnp
        import numpy as np
        D_MODEL = 128
        H = 16
        D_K = D_MODEL // H
        B, S, _ = q.shape

        def proj(x, w, b):
            y = x @ w.T + b
            return y.reshape(B, S, H, D_K).transpose(0, 2, 1, 3)
        Q = proj(q, wq_w, wq_b)
        K = proj(k, wk_w, wk_b)
        V = proj(v, wv_w, wv_b)
        scores = jnp.einsum('bhqd,bhkd->bhqk', Q, K) / jnp.sqrt(jnp.float32(D_K))
        scores = jnp.where(mask == 0, jnp.float32(1e-09), scores)
        attn = jax.nn.softmax(scores, axis=-1)
        out = jnp.einsum('bhqk,bhkd->bhqd', attn, V)
        out = out.transpose(0, 2, 1, 3).reshape(B, S, H * D_K)
        return out @ wo_w.T + wo_b

    def _L3_ffn_ref(x, w_gate, w_up, w_down):
        import jax, jax.numpy as jnp
        import numpy as np
        BLOCK = 32
        W_BITS = 4
        ACT_BITS = 16

        def act_qdq(x):
            qmax = 2.0 ** (ACT_BITS - 1) - 1.0
            scale = jnp.maximum(jnp.max(jnp.abs(x)) / qmax, 1e-12)
            return jnp.clip(jnp.round(x / scale), -qmax - 1.0, qmax) * scale

        def fixed_qdq_u16(x):
            scale = 1.0 / 65536.0
            return jnp.clip(jnp.round(x / scale), 0.0, 65535.0) * scale

        def lpbq_dequant(w):
            O, I = w.shape
            qmax = 2.0 ** (W_BITS - 1) - 1.0
            wb = w.reshape(O, I // BLOCK, BLOCK)
            s = jnp.maximum(jnp.max(jnp.abs(wb), axis=-1, keepdims=True) / qmax, 1e-12)
            wq = jnp.clip(jnp.round(wb / s), -qmax - 1.0, qmax) * s
            return wq.reshape(O, I)
        x = act_qdq(x)
        up = act_qdq(x @ lpbq_dequant(w_up).T)
        gate = act_qdq(x @ lpbq_dequant(w_gate).T)
        sig = fixed_qdq_u16(jax.nn.sigmoid(gate))
        gate = act_qdq(gate * sig)
        o = act_qdq(gate * up)
        return o @ lpbq_dequant(w_down).T
    x = x + _L0_xattn_ref(_layernorm(x, axis=-1), ctx_1024, ctx_1024, mask_1x1xSxS2_ik0, L0_xattn_wq_w, L0_xattn_wq_b, L0_xattn_wk_w, L0_xattn_wk_b, L0_xattn_wv_w, L0_xattn_wv_b, L0_xattn_out_w, L0_xattn_out_b)
    x = x + _L0_ffn_ref(_layernorm(x, axis=-1), L0_ffn_gate_w, L0_ffn_Wg, L0_ffn_Wu, L0_ffn_Wd)
    x = x + _L1_xattn_ref(_layernorm(x, axis=-1), ctx_1024, fside_1x1xSxS2_0, L1_xattn_wq, L1_xattn_wk, L1_xattn_wv, L1_xattn_wo)
    x = x + _L1_ffn_ref(_layernorm(x, axis=-1), L1_ffn_w_ln1, L1_ffn_Wq, L1_ffn_Wkva, L1_ffn_Wkvb, L1_ffn_Wo, L1_ffn_w_ln2, L1_ffn_Wgate, L1_ffn_expert_bias, L1_ffn_Wg, L1_ffn_Wu, L1_ffn_Wd, L1_ffn_sWg, L1_ffn_sWu, L1_ffn_sWd)
    x = x + _L2_xattn_ref(_layernorm(x, axis=-1), ctx_1024, ctx_1024, mask_1x1xSxS2_fk0, L2_xattn_Wq, L2_xattn_bq, L2_xattn_Wk, L2_xattn_bk, L2_xattn_Wv, L2_xattn_bv, L2_xattn_Wo, L2_xattn_bo)
    x = x + _L2_ffn_ref(_layernorm(x, axis=-1), L2_ffn_Wr, L2_ffn_br, L2_ffn_W1, L2_ffn_W3, L2_ffn_W2, L2_ffn_gamma, L2_ffn_beta)
    x = x + _L3_xattn_ref(_layernorm(x, axis=-1), ctx_1024, ctx_1024, mask_1x1xSxS2_ik1, L3_xattn_wq_w, L3_xattn_wq_b, L3_xattn_wk_w, L3_xattn_wk_b, L3_xattn_wv_w, L3_xattn_wv_b, L3_xattn_wo_w, L3_xattn_wo_b)
    x = x + _L3_ffn_ref(_layernorm(x, axis=-1), L3_ffn_w_gate, L3_ffn_w_up, L3_ffn_w_down)
    return x

_drawn_inputs = setup_inputs


def setup_inputs(seed=0):
    import zlib

    import numpy as np

    out = dict(_drawn_inputs(seed))
    spreads = {'L1_ffn_w_ln1': (1.0, 0.6),
     'L1_ffn_w_ln2': (1.0, 0.6),
     'L1_ffn_expert_bias': (0.0, 0.682),
     'L2_xattn_bq': (0.0, 2.0),
     'L2_xattn_bk': (0.0, 2.0),
     'L2_xattn_bv': (0.0, 0.8),
     'L2_xattn_bo': (0.0, 0.325),
     'L2_ffn_br': (0.0, 0.1),
     'L2_ffn_gamma': (1.0, 0.6),
     'L2_ffn_beta': (0.0, 0.645),
     'L3_xattn_wq_b': (0.0, 2.0),
     'L3_xattn_wk_b': (0.0, 2.0),
     'L3_xattn_wv_b': (0.0, 0.532),
     'L3_xattn_wo_b': (0.0, 0.436)}
    factors = {'fside_1x1xSxS2_0': 4.665,
     'L0_xattn_wq_w': 4.575,
     'L0_xattn_wq_b': 8.0,
     'L0_xattn_wk_w': 4.325,
     'L0_xattn_wk_b': 200.0,
     'L0_xattn_wv_b': 2.867,
     'L0_ffn_gate_w': 5.208,
     'L0_ffn_Wg': 4.578,
     'L0_ffn_Wu': 4.292,
     'L0_ffn_Wd': 4.354,
     'L1_xattn_wq': 8.0,
     'L1_xattn_wk': 8.0,
     'L1_ffn_Wq': 8.0,
     'L1_ffn_Wkva': 8.0,
     'L1_ffn_Wkvb': 8.0,
     'L1_ffn_Wo': 8.0,
     'L1_ffn_Wgate': 7.547,
     'L1_ffn_Wg': 5.917,
     'L1_ffn_Wu': 4.841,
     'L1_ffn_Wd': 6.453,
     'L1_ffn_sWg': 3.807,
     'L1_ffn_sWu': 3.869,
     'L1_ffn_sWd': 4.573,
     'L2_xattn_Wq': 48.35,
     'L2_xattn_Wk': 53.422,
     'L3_ffn_w_gate': 8.0,
     'L3_ffn_w_up': 8.0,
     'L3_ffn_w_down': 8.0,
     'L2_xattn_Wv': 5.168,
     'L2_xattn_Wo': 4.721}
    for name, (base, spread) in spreads.items():
        noise = np.random.default_rng([zlib.crc32(name.encode()), seed]).standard_normal(out[name].shape)
        drawn = base * np.exp(spread * noise) if base else spread * noise
        out[name] = jnp.asarray(drawn.astype(out[name].dtype))
    for name, factor in factors.items():
        out[name] = (out[name] * factor).astype(out[name].dtype)
    return out
```

```python
from contextlib import ExitStack, nullcontext

import concourse.bass as bass
from concourse import mybir

P = 128
D = 128
B, S = 8, 256
NT = B * S // P
PAIR = 2 * S
NPAIR = B // 2
TP = PAIR // P
H, HD = 16, 8
G = 4
HG = H // G
VW = HD + 1
EPS = 1e-5
BIG = 2.0 ** 46

ALU = mybir.AluOpType
ACT = mybir.ActivationFunctionType
F32 = mybir.dt.float32
BF16 = mybir.dt.bfloat16
I32 = mybir.dt.int32
X = mybir.AxisListType.X
NEG = -3.0e38
N_CHOSEN = 512 // 8 * 2


class Parts:
    pass


N_CONST = 4

ATTN_SEMS = """ln_partial ln_stats ln_msq pool_vare rstd_ready xn_ready xn_turned xnt_ready ctx_copied k_projected q_projected
    k_ready q_ready v_projected v_ready scores_ready masked max_ready p_ready p_turned pt_low_ready pt_high_ready
    values_weighed ot_ready ot_turned mi_read sum_inverted attn_ready attn_turned attnt_ready out_projected x_updated setup
    qbd_zeroed open_counted h_partial h_stats latent_projected latent_ready rope_projected rope_rotated rope_ready
    q_rotated q_odd_ready bq_scaled x_biased k_high_ready""".split()


def attention(nc, c, W, name, kind, loads=None):
    mla = kind == "mla"
    ident, ones_row = c.ident, c.ones_row
    SC, PT, PV, MI = c.SC, c.PT, c.PV, c.MI
    scale = 1.0 if kind == "alibi" else HD ** -0.5
    DUOS = H
    PER_B = DUOS // 2
    VD = 32 if mla else HD
    SLOT = 64 if mla else 32
    OT_H = P // SLOT
    OTS = 2 * H // OT_H
    VM = VD + 1 if mla else SLOT
    NA = H * VD // P
    JOBS = OTS + 4 * 2
    LATE = 5
    if mla:
        T_BLOCKS = ((0, 0), (0, 1), (1, 1))
    else:
        T_BLOCKS = ((0, 0), (0, 1), (1, 0), (1, 1))
    KEYS = (P, S) if mla else (S, S)

    def ot_of_step(st):
        u = st - 2
        return u // (OT_H // 2) if 0 <= u < DUOS and (u + 1) % (OT_H // 2) == 0 else None

    def tail_of_step(st):
        for b in range(2):
            qt = st - (PER_B * (b + 1) - 1) - (3 if mla else 4)
            if qt in (0, 1):
                return b, qt
        return None

    def mi_job(what, at):
        n = 0
        for st in range(DUOS + LATE):
            if tail_of_step(st) is not None:
                if (what, at) == ("turn_attn", tail_of_step(st)):
                    return n
                n += 1
            if tail_of_step(st) is not None:
                if (what, at) == ("project", tail_of_step(st)):
                    return n
                n += 1
            if ot_of_step(st) is not None:
                if (what, at) == ("turn_back", ot_of_step(st)):
                    return n
                n += 1

    with ExitStack() as scope:
        s = stage_sems(nc, scope, name, ATTN_SEMS)
        scope.callback(clear_sems, nc, s)

        def sb(nm, shape, dt=F32):
            return scope.enter_context(nc.sbuf_tensor(f"{name}_{nm}", shape, dt))

        A = Parts()
        A.st = sb("st", [P, NT, 6])
        A.mv = sb("mv", [P, NT, 2])
        A.vare = sb("vare", [P, NT])
        A.rstd = sb("rstd", [P, NT])
        A.xnt = sb("xnt", [P, NPAIR, PAIR])
        A.qbd = sb("qbd", [P, H, PAIR])
        A.kt = sb("kt", [P, PER_B if mla else G, PAIR])
        A.v = sb("v", [P, TP, H, VM])
        A.y = sb("y", [P, 2, 2, 2, S]) if kind != "alibi" else None
        def xn(tt):
            return A.y[:, tt // 8, tt // 4 % 2, tt // 2 % 2, tt % 2 * D:(tt % 2 + 1) * D] if mla else c.h[:, tt, :]

        A.mx = sb("mx", [P, 2, 2, 2])
        A.nmx = sb("nmx", [P, 2, 2, 2])
        A.p = sb("p", [P, 2, 2, 2, S])
        A.pt = sb("pt", [P, 2, 2, 4, P])
        A.ot = sb("ot", [P, S])
        A.rec = sb("rec", [P, 2, OT_H])
        A.attn = sb("attn", [P, 2, 2, H * VD])
        A.attnt = sb("attnt", [P, NA, P])
        A.m01 = sb("m01", [P, 2, S]) if kind in ("alibi", "mul") else None
        A.alibi = sb("alibi", [P, 2, S], BF16) if kind == "alibi" else None
        A.maskt_f = sb("maskt_f", [P, 2, S]) if kind == "alibi" else None
        A.open_k = sb("open_k", [P, S]) if kind == "alibi" else None
        A.open_q = sb("open_q", [P, 2, S]) if kind == "alibi" else None
        A.ctx = None if mla else sb("ctx", [P, PAIR])
        A.latent = sb("latent", [P, PAIR]) if mla else None
        A.rot = sb("rot", [P, 2, 2, PAIR]) if mla else None
        A.rope = sb("rope", [P, PAIR]) if mla else None
        A.msq = sb("msq", [P, NT]) if mla else None
        A.bq_scaled = sb("bq_scaled", [P, G]) if kind in ("add", "mul") else None
        block = scope.enter_context(nc.Block())

        if loads is not None:
            @block.sync
            def _(sp):
                loads(sp)

        @block.gpsimd
        def _(pool):
            nc.gpsimd.memset(A.v[:, :, :, :], 1.0).then_inc(s["qbd_zeroed"], 1)
            nc.gpsimd.memset(A.qbd[:, 0:H // 2, :], 0.0).then_inc(s["qbd_zeroed"], 1)
            if mla:
                nc.gpsimd.memset(A.ot[:, :], 0.0).then_inc(s["qbd_zeroed"], 1)
            pool.wait_ge(s["ln_stats"], NT)
            nc.gpsimd.tensor_scalar(A.vare[:, :], A.mv[:, :, 1], EPS, None, ALU.add).then_inc(s["pool_vare"], 1)
            pool.wait_ge(s["pool_vare"], 1)
            for m in range(NPAIR):
                tiles = slice(m * TP, m * TP + TP)
                nc.gpsimd.tensor_tensor(A.rstd[:, tiles], A.vare[:, tiles], c.mhalf[:, tiles], ALU.pow).then_inc(s["rstd_ready"], 1)
            nc.gpsimd.memset(A.qbd[:, H // 2:H, :], 0.0).then_inc(s["qbd_zeroed"], 1)
            if mla:
                pool.wait_ge(s["h_stats"], NT)
                nc.gpsimd.tensor_tensor(A.msq[:, :], A.mv[:, :, 0], A.mv[:, :, 0], ALU.mult).then_inc(s["ln_msq"], 1)
                pool.wait_ge(s["ln_msq"], 1)
                nc.gpsimd.tensor_tensor(A.vare[:, :], A.msq[:, :], A.mv[:, :, 1], ALU.add).then_inc(s["pool_vare"], 1)
                pool.wait_ge(s["pool_vare"], 2)
                nc.gpsimd.tensor_scalar(A.vare[:, :], A.vare[:, :], EPS, None, ALU.add).then_inc(s["pool_vare"], 1)
                pool.wait_ge(s["pool_vare"], 3)
                for m in range(NPAIR):
                    tiles = slice(m * TP, m * TP + TP)
                    nc.gpsimd.tensor_tensor(A.rstd[:, tiles], A.vare[:, tiles], c.mhalf[:, tiles], ALU.pow).then_inc(s["rstd_ready"], 1)
                pool.wait_ge(s["qbd_zeroed"], 4)
                with pool.Fori(0, NPAIR) as n:
                    for t in range(PER_B):
                        pool.wait_ge(s["q_rotated"], (n * PER_B + t + 1) * 2)
                        for i in range(2):
                            rows = slice(64 * i, 64 * i + 64)
                            ins_ = nc.gpsimd.tensor_tensor(A.qbd[rows, 2 * t + i, :], A.rot[rows, t % 2, 0, :],
                                                           A.rot[rows, t % 2, 1, :], ALU.add)
                        ins_.then_inc(s["q_ready"], 1)

        @block.tensor
        def _(pe):
            pe.wait_ge(W.loaded, W.n_loaded)
            if kind == "alibi":
                pe.wait_ge(c.const_ready, N_CONST)
                pe.wait_ge(s["setup"], 6)
                nc.tensor.matmul(MI[:, 0:S], c.ones_mat[:, :], A.open_k[:, :], start=True, stop=True).then_inc(s["open_counted"], 1)
            if not mla:
                pe.wait_ge(s["ctx_copied"], 1)
                for g, bank in enumerate((PT[:, 0, :], PT[:, 1, :], PV[:, :], MI[:, :])):
                    if g == 3 and kind == "alibi":
                        pe.wait_ge(s["setup"], 8)
                    nc.tensor.matmul(bank, W.wk[:, g, :], A.ctx[:, :], start=True, stop=True).then_inc(s["k_projected"], 1)
                for tt in range(TP):
                    ins_ = nc.tensor.matmul(SC[:, 3, tt * D:(tt + 1) * D], A.ctx[:, tt * P:(tt + 1) * P], W.wv[:, :],
                                            start=True, stop=True)
                ins_.then_inc(s["v_projected"], 1)
            for m in range(NPAIR):
                pe.wait_ge(s["xn_ready"], m * TP + TP)
                if m == 3 and not mla:
                    pe.wait_ge(s["v_ready"], 1)
                for tt in range(TP):
                    ins_ = nc.tensor.transpose(SC[:, m, tt * P:(tt + 1) * P], xn(m * TP + tt), ident[:, :])
                ins_.then_inc(s["xn_turned"], 1)
            pe.wait_ge(s["xnt_ready"], NPAIR)

            def attend(n, first=False, end=False):
                xnt = None if end else A.xnt[:, 0, :] if first else A.xnt[:, bass.ds(n, 1), :].rearrange("p o t -> p (o t)")

                def project_cross():
                    for g in range(G):
                        nc.tensor.matmul(SC[:, g, :], W.wq[:, g, :], xnt, start=True, stop=True).then_inc(s["q_projected"], 1)
                    if not first:
                        pe.wait_ge(s["ctx_copied"], n + 1)
                        pe.wait_ge(s["pt_low_ready"], n * DUOS)
                        pe.wait_ge(s["pt_high_ready"], n * DUOS)
                        for g, bank in enumerate((PT[:, 0, :], PT[:, 1, :], SC[:, 0, :], SC[:, 1, :])):
                            if g >= 2:
                                pe.wait_ge((s["q_ready"], s["q_ready"] if kind == "alibi" else s["q_odd_ready"])[g - 2],
                                           n * G + g - 1 if kind == "alibi" else n * 2 + 1)
                            nc.tensor.matmul(bank, W.wk[:, g, :], A.ctx[:, :], start=True, stop=True).then_inc(s["k_projected"], 1)
                        pe.wait_ge(s["q_ready"], n * G + 3 if kind == "alibi" else n * 2 + 2)
                        for tt in range(TP):
                            ins_ = nc.tensor.matmul(SC[:, 2, tt * D:(tt + 1) * D], A.ctx[:, tt * P:(tt + 1) * P], W.wv[:, :],
                                                    start=True, stop=True)
                        ins_.then_inc(s["v_projected"], 1)
                    pe.wait_ge(s["k_ready"], n * 2 + 2)
                    pe.wait_ge(s["k_high_ready"], n * 2 + 2)
                    if kind == "alibi":
                        pe.wait_ge(s["q_ready"], n * G + G)
                    else:
                        pe.wait_ge(s["q_ready"], n * 2 + 2)
                        pe.wait_ge(s["q_odd_ready"], n * 2 + 2)

                def project_latent():
                    if not first:
                        pe.wait_ge(s["ot_ready"], n * OTS)
                        pe.wait_ge(s["pt_low_ready"], n * DUOS)
                        pe.wait_ge(s["pt_high_ready"], n * DUOS)
                    nc.tensor.matmul(PV[:, :], W.wlat[:, :], xnt, start=True, stop=True).then_inc(s["latent_projected"], 1)
                    for k, w in enumerate((W.wkr, W.wks)):
                        ins_ = nc.tensor.matmul(PT[:, k, :], w[:, :], xnt, start=True, stop=True)
                    ins_.then_inc(s["rope_projected"], 1)
                    pe.wait_ge(s["latent_ready"], n + 1)
                    for t in range(PER_B):
                        if t >= 2:
                            pe.wait_ge(s["q_rotated"], (n * PER_B + t - 1) * 2)
                        for k, w in enumerate((W.wq, W.wqs)):
                            ins_ = nc.tensor.matmul(SC[:, t % 2 * 2 + k, :], w[:, t, :], xnt, start=True, stop=True)
                        ins_.then_inc(s["q_projected"], 1)
                        if t < TP:
                            if t >= 1:
                                pe.wait_ge(s["v_ready"], n * TP + t)
                            nc.tensor.matmul(PV[:, :], A.latent[:, t * P:(t + 1) * P], W.wvb[:, :], start=True, stop=True)\
                                .then_inc(s["v_projected"], 1)
                    pe.wait_ge(s["rope_rotated"], (n + 1) * 2)
                    for t in range(PER_B):
                        if t >= 2:
                            pe.wait_ge(s["k_ready"], n * PER_B + t - 1)
                        nc.tensor.matmul(PT[:, t % 2, :], W.wkb[:, t, :], A.latent[:, :], start=True, stop=True)\
                            .then_inc(s["k_projected"], 1)
                    pe.wait_ge(s["q_ready"], n * PER_B + PER_B)
                    pe.wait_ge(s["k_ready"], n * PER_B + PER_B)
                    pe.wait_ge(s["v_ready"], n * TP + TP)

                def scores(u):
                    b, hh = u // PER_B, u % PER_B * 2
                    if u == 1 and not mla:
                        pe.wait_ge(s["v_ready"], n + 1)
                    for i in range(2):
                        if u >= 2:
                            pe.wait_ge(s["p_ready"] if kind == "alibi" else s["masked"], (n * DUOS + u - 2) * 2 + i + 1)
                        h, bank = hh + i, u % 2 * 2 + i
                        for qt in range(2):
                            q0 = b * S + qt * P
                            out = SC[:, bank, qt * S:qt * S + KEYS[qt]]
                            ins_ = nc.tensor.matmul(out, A.qbd[:, h, q0:q0 + P],
                                                    A.kt[:, h // 2 if mla else h // HG, b * S:b * S + KEYS[qt]],
                                                    start=True, stop=kind != "alibi")
                            if kind == "alibi":
                                ins_ = nc.tensor.matmul(out, c.slope_ident[:, h, :], A.alibi[:, qt, :], start=False, stop=True)
                        ins_.then_inc(s["scores_ready"], 1)

                def turn_probs(u):
                    for i, evac in ((0, s["pt_low_ready"]), (1, s["pt_high_ready"])):
                        pe.wait_ge(s["p_ready"], (n * DUOS + u) * 2 + i + 1)
                        if u >= 1 or not first:
                            pe.wait_ge(evac, n * DUOS + u)
                        for t, (kt, qt) in enumerate(T_BLOCKS):
                            ins_ = nc.tensor.transpose(PT[:, i, t * P:(t + 1) * P], A.p[:, u % 2, i, qt, kt * P:(kt + 1) * P],
                                                       ident[:, :])
                        ins_.then_inc(s["p_turned"], 1)

                def weigh_values(u, n):
                    b, hh = u // PER_B, u % PER_B * 2
                    pe.wait_ge(s["pt_low_ready"], n * DUOS + u + 1)
                    pe.wait_ge(s["pt_high_ready"], n * DUOS + u + 1)
                    o = u // (OT_H // 2)
                    if u % (OT_H // 2) == 0 and (o >= 1 or not first):
                        pe.wait_ge(s["ot_ready"], n * OTS + o)
                    for kt in range(2):
                        for i in range(2):
                            h = hh + i
                            r0 = SLOT * (h % OT_H)
                            q0 = P if mla and kt == 1 else 0
                            src = A.pt[:, u % 2, i, 2 * kt:2 * kt + (S - q0) // P, :].rearrange("p b q -> p (b q)")
                            ins_ = nc.tensor.matmul(PV[r0:r0 + VM, q0:S], A.v[:, 2 * b + kt, h, :], src,
                                                    start=kt == 0, stop=kt == 1)
                    ins_.then_inc(s["values_weighed"], 1)

                def turn_back(o, n):
                    pe.wait_ge(s["ot_ready"], n * OTS + o + 1)
                    if mi_job("turn_back", o) or not first:
                        pe.wait_ge(s["mi_read"], n * JOBS + mi_job("turn_back", o))
                    for qt in range(2):
                        ins_ = nc.tensor.transpose(MI[:, qt * P:(qt + 1) * P], A.ot[:, qt * P:(qt + 1) * P], ident[:, :])
                    ins_.then_inc(s["ot_turned"], 1)

                def turn_attn(b, qt, n):
                    pe.wait_ge(s["attn_ready"], n * OTS + OTS // 2 * (b + 1))
                    pe.wait_ge(s["mi_read"], n * JOBS + mi_job("turn_attn", (b, qt)))
                    for a in range(NA):
                        ins_ = nc.tensor.transpose(MI[:, a * P:(a + 1) * P], A.attn[:, b, qt, a * P:(a + 1) * P], ident[:, :])
                    ins_.then_inc(s["attn_turned"], 1)

                def project_out(b, qt, n):
                    pe.wait_ge(s["attnt_ready"], n * TP + b * 2 + qt + 1)
                    pe.wait_ge(s["mi_read"], n * JOBS + mi_job("project", (b, qt)))
                    for a in range(NA):
                        ins_ = nc.tensor.matmul(MI[:, 0:D], A.attnt[:, a, :], W.wo[:, a, :], start=a == 0, stop=a == NA - 1)
                    ins_.then_inc(s["out_projected"], 1)

                def step(st, n):
                    if st < DUOS:
                        turn_probs(st)
                    if 1 <= st <= DUOS:
                        weigh_values(st - 1, n)
                    if tail_of_step(st) is not None:
                        project_out(*tail_of_step(st), n)
                    if ot_of_step(st) is not None:
                        turn_back(ot_of_step(st), n)

                if not first:
                    step(DUOS, n - 1)
                if not end:
                    (project_latent if mla else project_cross)()
                    scores(0)
                for st in range(LATE if end else DUOS):
                    late = st + DUOS + 1 if st < LATE and not first else 0
                    if not end and st + 1 < DUOS:
                        scores(st + 1)
                    for at, m in ((late, n - 1), (0 if end else st, n)):
                        if tail_of_step(at) is not None:
                            turn_attn(*tail_of_step(at), m)
                    if late:
                        step(late, n - 1)
                    if not end:
                        step(st, n)

            attend(0, first=True)
            with pe.Fori(1, NPAIR) as n:
                attend(n)
            attend(NPAIR, end=True)

        @block.vector
        def _(dve):
            dve.wait_ge(W.loaded, W.n_loaded)
            if kind in ("alibi", "mul"):
                nc.vector.tensor_scalar(A.m01[:, :, :], W.mask_i[:, :, :], 0.0, None, ALU.not_equal).then_inc(s["setup"], 1)
            if kind == "alibi":
                nc.vector.tensor_scalar(A.maskt_f[:, :, :], W.maskt_i[:, :, :], 0.0, None, ALU.not_equal).then_inc(s["setup"], 1)
                dve.wait_ge(s["setup"], 2)
                nc.vector.tensor_tensor(W.bias[:, :, :], W.bias[:, :, :], A.m01[:, :, :], ALU.mult).then_inc(s["setup"], 1)
                nc.vector.tensor_tensor(A.open_k[:, :], A.maskt_f[:, 0, :], A.maskt_f[:, 1, :], ALU.add).then_inc(s["setup"], 1)
                nc.vector.tensor_scalar(A.m01[:, :, :], A.m01[:, :, :], 1.0, BIG, ALU.subtract, ALU.mult).then_inc(s["setup"], 1)
                dve.wait_ge(s["setup"], 5)
                nc.vector.tensor_tensor(A.alibi[:, :, :], W.bias[:, :, :], A.m01[:, :, :], ALU.add).then_inc(s["setup"], 1)
                dve.wait_ge(s["open_counted"], 1)
                for b in range(2):
                    nc.vector.tensor_scalar(A.open_q[:, b, :], MI[:, 0:S], 0.0, None, ALU.is_gt).then_inc(s["setup"], 1)
                dve.wait_ge(s["setup"], 8)
            if kind == "mul":
                dve.wait_ge(s["setup"], 1)
            for tt in range(NT):
                nc.vector.bn_stats(A.st[:, tt, :], c.x[:, tt, :]).then_inc(s["ln_partial"], 1)
            dve.wait_ge(s["ln_partial"], NT)
            for tt in range(NT):
                nc.vector.bn_aggr(A.mv[:, tt, :], A.st[:, tt, :]).then_inc(s["ln_stats"], 1)
            dve.wait_ge(s["ln_stats"], NT)
            for tt in range(NT):
                if tt % TP == 0:
                    dve.wait_ge(s["rstd_ready"], tt // TP + 1)
                nc.vector.tensor_scalar(c.h[:, tt, :], c.x[:, tt, :], A.mv[:, tt, 0:1], A.rstd[:, tt:tt + 1], ALU.subtract, ALU.mult)\
                    .then_inc(s["h_partial" if mla else "xn_ready"], 1)
            if mla:
                dve.wait_ge(s["h_partial"], NT)
                for tt in range(NT):
                    nc.vector.bn_stats(A.st[:, tt, :], c.h[:, tt, :]).then_inc(s["h_partial"], 1)
                dve.wait_ge(s["h_partial"], 2 * NT)
                for tt in range(NT):
                    nc.vector.bn_aggr(A.mv[:, tt, :], A.st[:, tt, :]).then_inc(s["h_stats"], 1)
                for tt in range(NT):
                    if tt % TP == 0:
                        dve.wait_ge(s["rstd_ready"], NPAIR + tt // TP + 1)
                    nc.vector.tensor_scalar(xn(tt), c.h[:, tt, :], A.rstd[:, tt:tt + 1], None, ALU.mult)\
                        .then_inc(s["xn_ready"], 1)

            def values(n, bank):
                dve.wait_ge(s["v_projected"], n + 1)
                nc.vector.tensor_tensor(A.v[:, :, :, 0:HD], SC[:, bank, :].rearrange("p (t h w) -> p t h w", t=TP, h=H),
                                        W.brow[:, 0, :].rearrange("p (h w) -> p h w", h=H).unsqueeze(1).to_broadcast([P, TP, H, HD]),
                                        ALU.add).then_inc(s["v_ready"], 1)

            if not mla:
                dve.wait_ge(s["qbd_zeroed"], 1)
                values(0, 3)
            for m in range(0, NPAIR, 2):
                dve.wait_ge(s["xn_turned"], m + 1)
                if mla:
                    nc.vector.tensor_scalar(A.xnt[:, m, :], SC[:, m, :], W.w_ln[:, 0:1], None, ALU.mult).then_inc(s["xnt_ready"], 1)
                else:
                    nc.vector.tensor_copy(A.xnt[:, m, :], SC[:, m, :]).then_inc(s["xnt_ready"], 1)

            def attend(n, first=False, end=False):
                def queries_cross():
                    dve.wait_ge(s["qbd_zeroed"], 3)
                    for g in range(0, G, 1 if kind == "alibi" else 2):
                        dve.wait_ge(s["q_projected"], n * G + g + 1)
                        for j in range(HG):
                            rows = slice(32 * j, 32 * j + 32)
                            dst, src = A.qbd[rows, g * HG + j, :], SC[rows, g, :]
                            if kind == "alibi":
                                ins_ = nc.vector.scalar_tensor_tensor(dst, src, W.bq[rows, g:g + 1],
                                                                      A.open_q[rows, :, :].rearrange("p b s -> p (b s)"),
                                                                      ALU.add, ALU.mult)
                            else:
                                ins_ = nc.vector.tensor_scalar(dst, src, W.bq[rows, g:g + 1], scale, ALU.add, ALU.mult)
                        ins_.then_inc(s["q_ready"], 1)
                    if first:
                        nc.vector.tensor_tensor(c.x[:, :, :], c.x[:, :, :], W.brow[:, 1, :].unsqueeze(1).to_broadcast([P, NT, D]),
                                                ALU.add).then_inc(s["x_biased"], 1)
                        dve.wait_ge(s["x_biased"], 1)
                    else:
                        for g in range(2, G):
                            dve.wait_ge(s["k_projected"], n * G + g + 1)
                            nc.vector.tensor_scalar(A.kt[:, g, :], SC[:, g - 2, :], W.bk[:, g:g + 1], None, ALU.add)\
                                .then_inc(s["k_high_ready"], 1)
                        values(n, 2)

                def rotate():
                    dve.wait_ge(s["rope_projected"], n + 1)
                    for k in range(2):
                        nc.vector.tensor_tensor(A.rot[:, 0, k, :], PT[:, k, :], W.rope_k[:, k, :], ALU.mult).then_inc(s["rope_rotated"], 1)
                    dve.wait_ge(s["rope_rotated"], (n + 1) * 2)
                    nc.vector.tensor_tensor(A.rope[:, :], A.rot[:, 0, 0, :], A.rot[:, 0, 1, :], ALU.add).then_inc(s["rope_ready"], 1)
                    dve.wait_ge(s["rope_ready"], n + 1)
                    for t in range(PER_B):
                        dve.wait_ge(s["q_projected"], n * PER_B + t + 1)
                        if t >= 2:
                            dve.wait_ge(s["q_ready"], n * PER_B + t - 1)
                        for k in range(2):
                            nc.vector.tensor_tensor(A.rot[:, t % 2, k, :], SC[:, t % 2 * 2 + k, :], W.rope_q[:, k, :], ALU.mult)\
                                .then_inc(s["q_rotated"], 1)
                    for t in range(PER_B):
                        dve.wait_ge(s["k_projected"], n * PER_B + t + 1)
                        nc.vector.tensor_tensor(A.kt[:, t, :], PT[:, t % 2, :], A.rope[:, :], ALU.add).then_inc(s["k_ready"], 1)

                def mask_and_max(u):
                    for i in range(2):
                        dve.wait_ge(s["scores_ready"], (n * DUOS + u) * 2 + i + 1)
                        if kind == "alibi":
                            nc.vector.tensor_reduce(A.mx[:, u % 2, i, :], SC[:, u % 2 * 2 + i, :].rearrange("p (q k) -> p q k", q=2),
                                                    X, ALU.max).then_inc(s["masked"], 1)
                        else:
                            if u >= 2:
                                dve.wait_ge(s["p_ready"], (n * DUOS + u - 2) * 2 + i + 1)
                            dve.nop(nofuse=True)
                            for qt in range(2):
                                keys = KEYS[qt]
                                ins_ = nc.vector.tensor_tensor_reduce(
                                    A.y[:, u % 2, i, qt, 0:keys], SC[:, u % 2 * 2 + i, qt * S:qt * S + keys],
                                    A.m01[:, qt, 0:keys] if kind == "mul" else W.bias[:, qt, 0:keys], 1.0, NEG,
                                    ALU.mult if kind == "mul" else ALU.add, ALU.max, A.mx[:, u % 2, i, qt:qt + 1])
                            ins_.then_inc(s["masked"], 1)
                        dve.wait_ge(s["masked"], (n * DUOS + u) * 2 + i + 1)
                        if kind == "alibi" and u >= 2:
                            dve.wait_ge(s["p_ready"], (n * DUOS + u - 2) * 2 + i + 1)
                        nc.vector.tensor_scalar(A.nmx[:, u % 2, i, :], A.mx[:, u % 2, i, :], -1.0, None, ALU.mult)\
                            .then_inc(s["max_ready"], 1)

                def copy_turned(u, n):
                    dve.wait_ge(s["p_turned"], (n * DUOS + u) * 2 + 1)
                    if u >= 2:
                        dve.wait_ge(s["values_weighed"], n * DUOS + u - 1)
                    nb = len(T_BLOCKS)
                    nc.vector.tensor_copy(A.pt[:, u % 2, 0, 0:nb, :], PT[:, 0, 0:nb * P].rearrange("p (a c) -> p a c", a=nb))\
                        .then_inc(s["pt_low_ready"], 1)

                def normalise(o, n):
                    b, h0 = o // (OTS // 2), o % (OTS // 2) * OT_H
                    dve.wait_ge(s["ot_turned"], n * OTS + o + 1)
                    pv = MI[:, 0:2 * P].rearrange("p (q h w) -> p q h w", q=2, h=OT_H)
                    nc.vector.reciprocal(A.rec[:, :, :], pv[:, :, :, VD]).then_inc(s["sum_inverted"], 1)
                    dve.wait_ge(s["sum_inverted"], n * OTS + o + 1)
                    for qt in range(2):
                        ins_ = nc.vector.tensor_tensor(
                            A.attn[:, b, qt, h0 * VD:(h0 + OT_H) * VD].rearrange("p (h w) -> p h w", h=OT_H),
                            pv[:, qt, :, 0:VD], A.rec[:, qt, :].unsqueeze(2).to_broadcast([P, OT_H, VD]), ALU.mult)
                    ins_.then_inc(s["attn_ready"], 1)
                    dve.wait_ge(s["attn_ready"], n * OTS + o + 1)
                    dve.sem_inc(s["mi_read"], 1)

                def add_to_x(b, qt, n):
                    dve.wait_ge(s["out_projected"], n * TP + b * 2 + qt + 1)
                    xt = (c.h if mla else c.x)[:, n * TP + (b * 2 + qt), :]
                    nc.vector.tensor_tensor(xt, xt, MI[:, 0:D], ALU.add).then_inc(s["mi_read"], 1)

                def step(st, n):
                    if 1 <= st <= DUOS:
                        copy_turned(st - 1, n)
                    if tail_of_step(st - 1) is not None:
                        add_to_x(*tail_of_step(st - 1), n)
                    if ot_of_step(st - 1) is not None:
                        normalise(ot_of_step(st - 1), n)

                if not first:
                    step(DUOS, n - 1)
                if not end:
                    (rotate if mla else queries_cross)()
                for st in range(LATE if end else DUOS):
                    if not end:
                        mask_and_max(st)
                    if st < LATE and not first:
                        step(st + DUOS + 1, n - 1)
                    if not end:
                        step(st, n)

            attend(0, first=True)
            with dve.Fori(1, NPAIR) as n:
                attend(n)
            attend(NPAIR, end=True)

        @block.scalar
        def _(act):
            act.wait_ge(W.loaded, W.n_loaded)
            act.wait_ge(s["qbd_zeroed"], 3 if mla else 1)
            if kind in ("add", "mul"):
                nc.scalar.activation(A.bq_scaled[:, :], W.bq[:, :], ACT.Copy, scale=scale).then_inc(s["bq_scaled"], 1)
                act.wait_ge(s["bq_scaled"], 1)

            def copy_odd_norms():
                for m in range(1, NPAIR, 2):
                    act.wait_ge(s["xn_turned"], m + 1)
                    nc.scalar.activation(A.xnt[:, m, :], SC[:, m, :], ACT.Copy, scale=W.w_ln[:, 0:1] if mla else 1.0)\
                        .then_inc(s["xnt_ready"], 1)

            def attend(n, first=False, end=False):
                def latents_and_values():
                    if first:
                        copy_odd_norms()
                    act.wait_ge(s["latent_projected"], n + 1)
                    nc.scalar.copy(A.latent[:, :], PV[:, :]).then_inc(s["latent_ready"], 1)
                    for tt in range(TP):
                        act.wait_ge(s["v_projected"], n * TP + tt + 1)
                        nc.scalar.copy(A.v[:, tt, :, 0:VD], PV[:, :].rearrange("p (h w) -> p h w", h=H)).then_inc(s["v_ready"], 1)

                def queries_keys_values():
                    act.wait_ge(c.ctx_loaded, 16)
                    src = c.ctx[:, 0:PAIR] if first else c.ctx[:, bass.ts(n, PAIR)]
                    nc.scalar.copy(A.ctx[:, :], src).then_inc(s["ctx_copied"], 1)

                    def queries(g):
                        act.wait_ge(s["qbd_zeroed"], 3)
                        act.wait_ge(s["q_projected"], n * G + g + 1)
                        for j in range(HG):
                            rows = slice(32 * j, 32 * j + 32)
                            ins_ = nc.scalar.activation(A.qbd[rows, g * HG + j, :], SC[rows, g, :], ACT.Identity,
                                                        bias=A.bq_scaled[rows, g:g + 1], scale=scale)
                        ins_.then_inc(s["q_odd_ready"], 1)

                    if kind != "alibi" and not first:
                        queries(1)
                    for g, bank in enumerate((PT[:, 0, :], PT[:, 1, :]) + ((PV[:, :], MI[:, :]) if first else ())):
                        act.wait_ge(s["k_projected"], n * G + g + 1)
                        nc.scalar.activation(A.kt[:, g, :], bank, ACT.Identity, bias=W.bk[:, g:g + 1])\
                            .then_inc(s["k_ready"] if g < 2 else s["k_high_ready"], 1)
                    if kind != "alibi" and not first:
                        queries(3)
                    if first:
                        copy_odd_norms()
                    if kind != "alibi" and first:
                        queries(1)
                        queries(3)

                def exponentials(u):
                    for i in range(2):
                        act.wait_ge(s["max_ready"], (n * DUOS + u) * 2 + i + 1)
                        if u >= 2:
                            act.wait_ge(s["p_turned"], (n * DUOS + u - 2) * 2 + i + 1)
                        for qt in range(2):
                            keys = KEYS[qt]
                            src = (SC[:, u % 2 * 2 + i, qt * S:qt * S + keys] if kind == "alibi"
                                   else A.y[:, u % 2, i, qt, 0:keys])
                            ins_ = nc.scalar.activation(A.p[:, u % 2, i, qt, 0:keys], src, ACT.Exp, bias=A.nmx[:, u % 2, i, qt:qt + 1])
                        ins_.then_inc(s["p_ready"], 1)

                def copy_turned(u, n):
                    act.wait_ge(s["p_turned"], (n * DUOS + u) * 2 + 2)
                    if u >= 2:
                        act.wait_ge(s["values_weighed"], n * DUOS + u - 1)
                    nb = len(T_BLOCKS)
                    nc.scalar.copy(A.pt[:, u % 2, 1, 0:nb, :], PT[:, 1, 0:nb * P].rearrange("p (a c) -> p a c", a=nb))\
                        .then_inc(s["pt_high_ready"], 1)

                def copy_product(o, n):
                    act.wait_ge(s["values_weighed"], n * DUOS + (o + 1) * (OT_H // 2))
                    if o >= 1 or not first:
                        act.wait_ge(s["ot_turned"], n * OTS + o)
                    if not mla:
                        ins_ = nc.scalar.copy(A.ot[:, :], PV[:, 0:S])
                    else:
                        for j in range(OT_H):
                            rows = slice(SLOT * j, SLOT * j + VM)
                            ins_ = nc.scalar.copy(A.ot[rows, :], PV[rows, 0:S])
                    ins_.then_inc(s["ot_ready"], 1)

                def copy_attn(b, qt, n):
                    act.wait_ge(s["attn_turned"], n * TP + b * 2 + qt + 1)
                    nc.scalar.copy(A.attnt[:, :, :], MI[:, 0:NA * P].rearrange("p (a q) -> p a q", a=NA)).then_inc(s["attnt_ready"], 1)
                    act.wait_ge(s["attnt_ready"], n * TP + b * 2 + qt + 1)
                    act.sem_inc(s["mi_read"], 1)

                def step(st, n):
                    if 1 <= st <= DUOS:
                        copy_turned(st - 1, n)
                    if tail_of_step(st) is not None:
                        copy_attn(*tail_of_step(st), n)
                    if ot_of_step(st) is not None and not (mla and st > DUOS):
                        copy_product(ot_of_step(st), n)
                    if mla and st == DUOS:
                        copy_product(OTS - 1, n)

                if not first:
                    step(DUOS, n - 1)
                if not end:
                    (latents_and_values if mla else queries_keys_values)()
                for st in range(LATE if end else DUOS):
                    if not end:
                        exponentials(st)
                    if st < LATE and not first:
                        step(st + DUOS + 1, n - 1)
                    if not end:
                        step(st, n)

            attend(0, first=True)
            with act.Fori(1, NPAIR) as n:
                attend(n)
            attend(NPAIR, end=True)


def stage_sems(nc, scope, name, names):
    return {n: scope.enter_context(nc.semaphore(f"{name}_{n}")) for n in names}


def clear_sems(nc, s):
    with nc.Block() as block:
        @block.gpsimd
        def _(pool):
            for one in s.values():
                pool.sem_clear(one)


def loop(eng, count):
    return eng.Fori(0, count) if count > 1 else nullcontext(0)


def gate_tokens(nc, c, s, A, kind, src, xn, xnt, w_gate, w_col, E, loaded, n_loaded, bias_row=None):
    GROUPS = NT // TP
    with nc.Block() as block:
        @block.gpsimd
        def _(pool):
            for g in range(GROUPS):
                tiles = slice(g * TP, g * TP + TP)
                pool.wait_ge(s["stats"], g * TP + TP)
                if kind == "rms":
                    nc.gpsimd.tensor_tensor(A.msq[:, tiles], A.mv[:, tiles, 0], A.mv[:, tiles, 0], ALU.mult).then_inc(s["msq"], 1)
                    pool.wait_ge(s["msq"], g + 1)
                    nc.gpsimd.tensor_tensor(A.vare[:, tiles], A.msq[:, tiles], A.mv[:, tiles, 1], ALU.add).then_inc(s["vare"], 1)
                    pool.wait_ge(s["vare"], g * 2 + 1)
                    nc.gpsimd.tensor_scalar(A.vare[:, tiles], A.vare[:, tiles], EPS, None, ALU.add).then_inc(s["vare"], 1)
                    pool.wait_ge(s["vare"], g * 2 + 2)
                else:
                    nc.gpsimd.tensor_scalar(A.vare[:, tiles], A.mv[:, tiles, 1], EPS, None, ALU.add).then_inc(s["vare"], 1)
                    pool.wait_ge(s["vare"], g + 1)
                nc.gpsimd.tensor_tensor(A.rstd[:, tiles], A.vare[:, tiles], c.mhalf[:, 0:TP], ALU.pow).then_inc(s["rstd"], 1)

        @block.vector
        def _(dve):
            for t in range(NT):
                nc.vector.bn_stats(A.st[:, t, :], src[:, t, :]).then_inc(s["partial"], 1)
            for t in range(NT):
                dve.wait_ge(s["partial"], t + 1)
                nc.vector.bn_aggr(A.mv[:, t, :], A.st[:, t, :]).then_inc(s["stats"], 1)
            dve.wait_ge(s["stats"], NT)
            for t in range(NT):
                if t % TP == 0:
                    dve.wait_ge(s["rstd"], t // TP + 1)
                if kind == "rms":
                    ins_ = nc.vector.tensor_scalar(xn[:, t, :], src[:, t, :], A.rstd[:, t:t + 1], None, ALU.mult)
                else:
                    ins_ = nc.vector.tensor_scalar(xn[:, t, :], src[:, t, :], A.mv[:, t, 0:1], A.rstd[:, t:t + 1],
                                                   ALU.subtract, ALU.mult)
                ins_.then_inc(s["xn"], 1)
            dve.wait_ge(s["logits"], 1)
            nc.vector.tensor_copy(A.logits[:, :, :], c.PV[:, 0:NT * E].rearrange("p (t e) -> p t e", t=NT)).then_inc(s["logits_out"], 1)

        @block.scalar
        def _(act):
            if w_col is not None:
                act.wait_ge(loaded, n_loaded)
            for g in range(GROUPS):
                act.wait_ge(s["turned"], g + 1)
                nc.scalar.activation(xnt[:, g * PAIR:(g + 1) * PAIR], c.SC[:, g, :], ACT.Copy,
                                     scale=1.0 if w_col is None else w_col).then_inc(s["xnt"], 1)

        @block.tensor
        def _(pe):
            pe.wait_ge(loaded, n_loaded)
            for g in range(GROUPS):
                pe.wait_ge(s["xn"], g * TP + TP)
                for tt in range(TP):
                    ins_ = nc.tensor.transpose(c.SC[:, g, tt * P:(tt + 1) * P], xn[:, g * TP + tt, :], c.ident[:, :])
                ins_.then_inc(s["turned"], 1)
            for t in range(NT):
                if t % TP == 0:
                    pe.wait_ge(s["xnt"], t // TP + 1)
                ins_ = nc.tensor.matmul(c.PV[:, t * E:(t + 1) * E], xnt[:, t * P:(t + 1) * P], w_gate,
                                        start=True, stop=bias_row is None)
                if bias_row is not None:
                    ins_ = nc.tensor.matmul(c.PV[:, t * E:(t + 1) * E], c.ones_row[:, :], bias_row, start=False, stop=True)
            ins_.then_inc(s["logits"], 1)


def softmax_over_experts(nc, dve, s, A, E):
    def bc(t):
        return t[:, :].unsqueeze(2).to_broadcast([P, NT, E])
    nc.vector.tensor_reduce(A.r1[:, :], A.logits[:, :, :], X, ALU.max).then_inc(s["chain"], 1)
    dve.wait_ge(s["chain"], 1)
    nc.vector.tensor_tensor(A.prob[:, :, :], A.logits[:, :, :], bc(A.r1), ALU.subtract).then_inc(s["shifted"], 1)
    dve.wait_ge(s["exped"], 1)
    nc.vector.tensor_reduce(A.r1[:, :], A.prob[:, :, :], X, ALU.add).then_inc(s["chain"], 1)
    dve.wait_ge(s["chain"], 2)
    nc.vector.reciprocal(A.r2[:, :], A.r1[:, :]).then_inc(s["chain"], 1)
    dve.wait_ge(s["chain"], 3)
    nc.vector.tensor_tensor(A.prob[:, :, :], A.prob[:, :, :], bc(A.r2), ALU.mult).then_inc(s["chain"], 1)
    dve.wait_ge(s["chain"], 4)


def exp_of_shifted(nc, act, s, A):
    act.wait_ge(s["shifted"], 1)
    nc.scalar.activation(A.prob[:, :, :], A.prob[:, :, :], ACT.Exp).then_inc(s["exped"], 1)


def choose_tokens(nc, c, s, A, E):
    CAP = N_CHOSEN
    ROWS = B * E
    MI, PT = c.MI, c.PT
    with nc.Block() as block:
        @block.vector
        def _(dve):
            softmax_over_experts(nc, dve, s, A, E)
            for h in range(2):
                nc.vector.tensor_copy(A.cols[:, h, :, :], A.prob[:, h:NT:2, :]).then_inc(s["cols"], 1)
            dve.wait_ge(s["rows_turned"], 1)
            nc.vector.tensor_copy(A.rows[:, :], MI[0:ROWS, 0:S]).then_inc(s["chain"], 1)
            nc.vector.tensor_copy(A.left[:, :], MI[0:ROWS, 0:S]).then_inc(s["chain"], 1)
            dve.wait_ge(s["chain"], 6)
            for r in range(CAP // 8):
                nc.vector.max(A.top8[:, :], A.left[:, :]).then_inc(s["chain"], 1)
                dve.wait_ge(s["chain"], 7 + 2 * r)
                nc.vector.match_replace(A.left[:, :], A.top8[:, :], A.left[:, :], -1.0).then_inc(s["chain"], 1)
                dve.wait_ge(s["chain"], 8 + 2 * r)
            n = 6 + 2 * (CAP // 8)
            nc.vector.tensor_scalar(A.left[:, :], A.left[:, :], 0.0, None, ALU.is_lt).then_inc(s["chain"], 1)
            dve.wait_ge(s["chain"], n + 1)
            nc.vector.tensor_tensor(A.rows[:, :], A.rows[:, :], A.left[:, :], ALU.mult).then_inc(s["gate_rows"], 1)
            dve.wait_ge(s["cols_turned"], 1)
            for h in range(2):
                nc.vector.tensor_copy(A.gate[:, h:NT:2, :], PT[:, h, 0:ROWS].rearrange("p (b e) -> p b e", b=B)).then_inc(s["gates"], 1)

        @block.scalar
        def _(act):
            exp_of_shifted(nc, act, s, A)

        @block.tensor
        def _(pe):
            pe.wait_ge(s["cols"], 2)
            for h in range(2):
                ins_ = nc.tensor.transpose(MI[0:ROWS, h * P:(h + 1) * P], A.cols[:, h, :, :].rearrange("p b e -> p (b e)"),
                                           c.ident[:, :])
            ins_.then_inc(s["rows_turned"], 1)
            pe.wait_ge(s["gate_rows"], 1)
            for h in range(2):
                ins_ = nc.tensor.transpose(PT[:, h, 0:ROWS], A.rows[:, h * P:(h + 1) * P], c.ident[0:ROWS, 0:ROWS])
            ins_.then_inc(s["cols_turned"], 1)


def choose_experts(nc, c, s, A, E, shared):
    def bc(t):
        return t[:, :].unsqueeze(2).to_broadcast([P, NT, E])

    def order():
        return c.order[:, 0:E].unsqueeze(1).to_broadcast([P, NT, E])

    with nc.Block() as block:
        @block.vector
        def _(dve):
            softmax_over_experts(nc, dve, s, A, E)
            n = 4
            for src, hot, mx in ((A.prob, A.hot1, A.r1), (A.rest, A.hot2, A.r2)):
                if hot is A.hot2:
                    nc.vector.scalar_tensor_tensor(A.rest[:, :, :], A.hot1[:, :, :], -2.0, A.prob[:, :, :], ALU.mult, ALU.add)\
                        .then_inc(s["chain"], 1)
                    n += 1
                    dve.wait_ge(s["chain"], n)
                nc.vector.tensor_reduce(mx[:, :], src[:, :, :], X, ALU.max).then_inc(s["chain"], 1)
                dve.wait_ge(s["chain"], n + 1)
                nc.vector.tensor_tensor(hot[:, :, :], src[:, :, :], bc(mx), ALU.is_equal).then_inc(s["chain"], 1)
                dve.wait_ge(s["chain"], n + 2)
                nc.vector.tensor_tensor(hot[:, :, :], hot[:, :, :], order(), ALU.mult).then_inc(s["chain"], 1)
                dve.wait_ge(s["chain"], n + 3)
                nc.vector.tensor_reduce(A.r3[:, :], hot[:, :, :], X, ALU.max).then_inc(s["chain"], 1)
                dve.wait_ge(s["chain"], n + 4)
                nc.vector.tensor_tensor(hot[:, :, :], hot[:, :, :], bc(A.r3), ALU.is_equal).then_inc(s["chain"], 1)
                n += 5
                dve.wait_ge(s["chain"], n)
            nc.vector.tensor_tensor(A.rest[:, :, :], A.hot1[:, :, :], A.hot2[:, :, :], ALU.add).then_inc(s["chain"], 1)
            nc.vector.tensor_tensor(A.r3[:, :], A.r1[:, :], A.r2[:, :], ALU.add).then_inc(s["chain"], 1)
            dve.wait_ge(s["chain"], n + 2)
            nc.vector.reciprocal(A.r4[:, :], A.r3[:, :]).then_inc(s["chain"], 1)
            if shared:
                nc.vector.tensor_tensor(A.rest[:, :, :], A.rest[:, :, :], A.prob[:, :, :], ALU.mult).then_inc(s["chain"], 1)
                dve.wait_ge(s["chain"], n + 4)
                nc.vector.tensor_tensor(A.gate[:, :, 0:E], A.rest[:, :, :], bc(A.r4), ALU.mult).then_inc(s["gates"], 1)
            else:
                dve.wait_ge(s["chain"], n + 3)
                nc.vector.tensor_tensor(A.w1[:, :], A.r1[:, :], A.r4[:, :], ALU.mult).then_inc(s["gates"], 1)
                nc.vector.tensor_tensor(A.w2[:, :], A.r2[:, :], A.r4[:, :], ALU.mult).then_inc(s["gates"], 1)
            if shared:
                nc.vector.memset(A.gate[:, :, E:E + 1], 1.0).then_inc(s["gates"], 1)
                nc.vector.memset(A.gate[:, :, E + 1:E + 2], 0.0).then_inc(s["gates"], 1)

        @block.scalar
        def _(act):
            exp_of_shifted(nc, act, s, A)


def run_experts(nc, name, c, s, A, n_exp, unroll, IT, src, dst, subs=1, ln=None):
    CH = NT // TP
    UNITS = unroll * CH
    SC, PT = c.SC, c.PT
    n_it = n_exp // unroll

    with nc.Block() as block:
        @block.sync
        def _(sp):
            with loop(sp, n_it) as it:
                for r in range(unroll):
                    e = it * unroll + r
                    sp.wait_ge(s["down"], e * CH + CH)
                    for t, w in ((A.wg, src["wg"]), (A.wu, src["wu"]), (A.wd, src["wd"])):
                        sp.dma_start(t[:, r % 2, :, :], w[bass.ds(e, 1)].rearrange("o p i n -> (o p) i n"))\
                            .then_inc((s["w_even"], s["w_odd"])[r % 2], 16)

        @block.tensor
        def _(pe):
            pe.sem_inc(s["down"], 2 * CH)
            with loop(pe, n_it) as it:
                def gate_up(t):
                    r, ch = t // CH, t % CH
                    if ch == 0:
                        pe.wait_ge((s["w_even"], s["w_odd"])[r % 2], (it * (unroll // 2) + r // 2 + 1) * 48)
                    for i in range(IT):
                        k = it * (UNITS * IT) + (t * IT + i)
                        pe.wait_ge(s["h_ready"], k + 1)
                        bank = 2 * ((t * IT + i) % 2)
                        x = c.xnt[:, ch * PAIR:(ch + 1) * PAIR]
                        nc.tensor.matmul(SC[:, bank, :], A.wg[:, r % 2, i, :], x, start=True, stop=True)
                        nc.tensor.matmul(SC[:, bank + 1, :], A.wu[:, r % 2, i, :], x, start=True, stop=True).then_inc(s["gu"], 1)

                def down(t):
                    r = t // CH
                    pe.wait_ge(s["h_ready"], it * (UNITS * IT) + (t + 1) * IT + 2)
                    pe.wait_ge(s["added"], it * UNITS + t + (2 if subs == 2 else 1))
                    for tt in range(TP):
                        for sub in range(subs):
                            bank = sub if subs == 2 else t % 2
                            rows = slice(64 * sub, 64 * sub + 64) if subs == 2 else slice(0, P)
                            for i in range(IT):
                                ins_ = nc.tensor.matmul(PT[:, bank, tt * D:(tt + 1) * D], A.h[rows, t % 2, i, tt * P:(tt + 1) * P],
                                                        A.wd[rows, r % 2, i, :], start=i == 0, stop=i == IT - 1)
                    ins_.then_inc(s["down"], 1)

                for t in range(UNITS + 1):
                    if t < UNITS:
                        gate_up(t)
                    if t >= 1:
                        down(t - 1)

        @block.scalar
        def _(act):
            with loop(act, n_it) as it:
                for k in range(UNITS * IT):
                    act.wait_ge(s["gu"], it * (UNITS * IT) + k + 1)
                    act.wait_ge(s["h_ready"], it * (UNITS * IT) + k + 1)
                    nc.scalar.activation(A.sg[:, k % 2, :], SC[:, 2 * (k % 2), :], ACT.Silu).then_inc(s["silu"], 1)

        @block.vector
        def _(dve):
            dve.sem_inc(s["h_ready"], 2)
            dve.sem_inc(s["added"], 2)
            with loop(dve, n_it) as it:
                def hidden(t):
                    for i in range(IT):
                        k = t * IT + i
                        dve.wait_ge(s["silu"], it * (UNITS * IT) + k + 1)
                        if i == 0:
                            dve.wait_ge(s["down"], it * UNITS + t - 1 + 2 * CH)
                        nc.vector.tensor_tensor(A.h[:, t % 2, i, :], A.sg[:, k % 2, :], SC[:, 2 * (k % 2) + 1, :], ALU.mult)\
                            .then_inc(s["h_ready"], 1)

                def add(t):
                    r, ch = t // CH, t % CH
                    dve.wait_ge(s["down"], it * UNITS + t + 1 + 2 * CH)
                    for tt in range(TP):
                        tile = ch * TP + tt
                        for sub in range(subs):
                            if subs == 2 and sub == 1:
                                dve.wait_ge(s["half_added"], it * (UNITS * TP) + t * TP + tt + 1)
                            bank = sub if subs == 2 else t % 2
                            col = bass.ds((it * unroll + r) * subs + sub, 1)
                            ins_ = nc.vector.scalar_tensor_tensor(dst[:, tile, :], PT[:, bank, tt * D:(tt + 1) * D],
                                                                  A.gate[:, tile, col], dst[:, tile, :], ALU.mult, ALU.add)
                            if subs == 2 and sub == 0:
                                ins_.then_inc(s["half_added"], 1)
                    ins_.then_inc(s["added"], 1)

                for t in range(UNITS + 1):
                    if t < UNITS:
                        hidden(t)
                    if t >= 1:
                        add(t - 1)


GATE_SEMS = "partial stats msq vare rstd xn turned xnt logits logits_out".split()
ROUTE_SEMS = "chain shifted exped cols rows_turned gate_rows cols_turned gates".split()
EXPERT_SEMS = "down h_ready added half_added gu silu w_even w_odd".split()


def moe_tiles(sb, name, E, n_col, IT):
    A = Parts()
    A.st = sb(f"{name}_st", [P, NT, 6])
    A.mv = sb(f"{name}_mv", [P, NT, 2])
    A.msq = sb(f"{name}_msq", [P, NT])
    A.vare = sb(f"{name}_vare", [P, NT])
    A.rstd = sb(f"{name}_rstd", [P, NT])
    A.logits = sb(f"{name}_logits", [P, NT, E])
    A.prob = sb(f"{name}_prob", [P, NT, E])
    A.r1 = sb(f"{name}_r1", [P, NT])
    A.r2 = sb(f"{name}_r2", [P, NT])
    A.gate = sb(f"{name}_gate", [P, NT, n_col])
    A.wg = sb(f"{name}_wg", [P, 2, IT, P])
    A.wu = sb(f"{name}_wu", [P, 2, IT, P])
    A.wd = sb(f"{name}_wd", [P, 2, IT, D])
    A.sg = sb(f"{name}_sg", [P, 2, PAIR])
    A.h = sb(f"{name}_h", [P, 2, IT, PAIR])
    return A


def expert_choice_ffn(nc, c, a, W):
    E = 8
    with ExitStack() as scope:
        def sb(name, shape, dt=F32):
            return scope.enter_context(nc.sbuf_tensor(name, shape, dt))
        A = moe_tiles(sb, "F0", E, E, 2)
        A.cols, A.rows = sb("F0_cols", [P, 2, B, E]), sb("F0_rows", [B * E, S])
        A.left, A.top8 = sb("F0_left", [B * E, S]), sb("F0_top8", [B * E, 8])
        c.xnt = sb("F0_xnt", [P, B * S])
        s = stage_sems(nc, scope, "F0", GATE_SEMS + ROUTE_SEMS + EXPERT_SEMS)
        scope.callback(clear_sems, nc, s)
        gate_tokens(nc, c, s, A, "ln", c.x, c.h, c.xnt, W.gate[:, :], None, E, W.loaded, W.n_loaded)
        choose_tokens(nc, c, s, A, E)
        run_experts(nc, "F0", c, s, A, E, 2, 2, {"wg": a["F0_wg"], "wu": a["F0_wu"], "wd": a["F0_wd"]}, c.x)


def shared_and_routed_ffn(nc, c, a, W):
    E, PAIRS = 8, 5
    with ExitStack() as scope:
        def sb(name, shape, dt=F32):
            return scope.enter_context(nc.sbuf_tensor(name, shape, dt))
        A = moe_tiles(sb, "F1", E, 2 * PAIRS, 1)
        A.hot1, A.hot2, A.rest = sb("F1_hot1", [P, NT, E]), sb("F1_hot2", [P, NT, E]), sb("F1_rest", [P, NT, E])
        A.r3, A.r4 = sb("F1_r3", [P, NT]), sb("F1_r4", [P, NT])
        s = stage_sems(nc, scope, "F1", GATE_SEMS + ROUTE_SEMS + EXPERT_SEMS)
        scope.callback(clear_sems, nc, s)
        c.xnt = sb("F1_xnt", [P, B * S])
        A.xn = sb("F1_xn", [P, NT, D])
        gate_tokens(nc, c, s, A, "rms", c.h, A.xn, c.xnt, W.gate[:, :], W.w_ln[:, 0:1], E, W.loaded, W.n_loaded, W.bias[:, :])
        choose_experts(nc, c, s, A, E, True)
        run_experts(nc, "F1", c, s, A, PAIRS, PAIRS, 1, {"wg": a["F1_wg"], "wu": a["F1_wu"], "wd": a["F1_wd"]}, c.h, subs=2)
        with nc.Block() as block:
            @block.vector
            def _(dve):
                nc.vector.tensor_tensor(c.x[:, :, :], c.x[:, :, :], c.h[:, :, :], ALU.add).then_inc(s["gates"], 1)


PLACE_SEMS = """consts0 placed counted scanned rows_zeroed scattered xs_loaded xs_turned xt_ready gu silu h_ready h_turned ht_ready
    y_ready y_stats y_moments y_rstd y_vare y_normed y_scaled ys_ready ys_stored y_added consts weights""".split()
GATHERED = ["gathered0", "gathered1", "gathered2", "gathered3"]
E2, F2 = 16, 512
ROUTED = 2 * B * S
TILES = ROUTED // P + E2
UNROLL = 16
MAGIC = 1.5 * 2.0 ** 23


def place_rows(nc, c, s, A):
    PV, MI = c.PV, c.MI
    with nc.Block() as block:
        @block.gpsimd
        def _(pool):
            nc.gpsimd.memset(A.tri[:, :], 0.0).then_inc(s["consts"], 1)
            nc.gpsimd.memset(A.ones_bf[:, :], 1.0).then_inc(s["consts"], 1)
            pool.wait_ge(s["consts"], 2)
            nc.gpsimd.affine_select(out=A.tri[:, :], in_=A.tri[:, :], compare_op=ALU.is_ge, fill=1.0, base=0,
                                    pattern=[[-1, P]], channel_multiplier=1).then_inc(s["consts"], 1)

        @block.tensor
        def _(pe):
            pe.wait_ge(s["consts"], 3)
            pe.wait_ge(s["placed"], 1)
            both = A.both[:, :, :].rearrange("p t e -> p (t e)")
            nc.tensor.matmul(PV[:, 0:NT * E2], A.tri[:, :], both, start=True, stop=True)
            nc.tensor.matmul(MI[:, 0:NT * E2], A.ones_bf[:, :], both, start=True, stop=True).then_inc(s["counted"], 1)

        @block.vector
        def _(dve):
            nc.vector.tensor_copy(A.both[:, :, :], A.rest[:, :, :]).then_inc(s["placed"], 1)
            nc.vector.memset(A.base[:, 0, :], 0.0).then_inc(s["scanned"], 1)
            nc.vector.memset(A.start[:, 0:1], 0.0).then_inc(s["scanned"], 1)
            dve.wait_ge(s["counted"], 1)
            nc.vector.tensor_copy(A.totals[:, :, :], MI[:, 0:NT * E2].rearrange("p (t e) -> p t e", t=NT)).then_inc(s["scanned"], 1)
            n = 3
            for t in range(NT):
                dve.wait_ge(s["scanned"], n)
                nc.vector.tensor_tensor(A.base[:, t + 1, :], A.base[:, t, :], A.totals[:, t, :], ALU.add).then_inc(s["scanned"], 1)
                n += 1
            dve.wait_ge(s["scanned"], n)
            nc.vector.tensor_scalar(A.need[:, :], A.base[:, NT, :], 1.0 / P, (P - 1) / (2.0 * P), ALU.mult, ALU.add)\
                .then_inc(s["scanned"], 1)
            dve.wait_ge(s["scanned"], n + 1)
            nc.vector.tensor_scalar(A.need[:, :], A.need[:, :], MAGIC, None, ALU.add).then_inc(s["scanned"], 1)
            dve.wait_ge(s["scanned"], n + 2)
            nc.vector.tensor_scalar(A.need[:, :], A.need[:, :], MAGIC, None, ALU.subtract).then_inc(s["scanned"], 1)
            n += 3
            for e in range(E2):
                dve.wait_ge(s["scanned"], n)
                nc.vector.tensor_tensor(A.start[:, e + 1:e + 2], A.start[:, e:e + 1], A.need[:, e:e + 1], ALU.add).then_inc(s["scanned"], 1)
                n += 1
            dve.wait_ge(s["scanned"], n)
            nc.vector.tensor_tensor(A.ended[:, :, :], A.start[:, 1:E2 + 1].unsqueeze(1).to_broadcast([P, TILES, E2]),
                                    c.count[:, 0:TILES].unsqueeze(2).to_broadcast([P, TILES, E2]), ALU.is_le).then_inc(s["scanned"], 1)
            nc.vector.tensor_scalar(A.need[:, :], A.start[:, 0:E2], float(P), None, ALU.mult).then_inc(s["scanned"], 1)
            nc.vector.tensor_tensor(A.base[:, 0:NT, :], A.base[:, 0:NT, :],
                                    PV[:, 0:NT * E2].rearrange("p (t e) -> p t e", t=NT), ALU.add).then_inc(s["scanned"], 1)
            dve.wait_ge(s["scanned"], n + 3)
            nc.vector.tensor_reduce(A.expert_f[:, :], A.ended[:, :, :], X, ALU.add).then_inc(s["scanned"], 1)
            nc.vector.tensor_tensor(A.base[:, 0:NT, :], A.base[:, 0:NT, :],
                                    A.need[:, :].unsqueeze(1).to_broadcast([P, NT, E2]), ALU.add).then_inc(s["scanned"], 1)
            dve.wait_ge(s["scanned"], n + 5)
            nc.vector.tensor_scalar(A.expert[:, :], A.expert_f[:, :], float(E2 - 1), None, ALU.min).then_inc(s["placed"], 1)
            n += 5
            for slot, hot in enumerate((A.hot1, A.hot2)):
                nc.vector.tensor_tensor(hot[:, :, :], hot[:, :, :], A.base[:, 0:NT, :], ALU.mult).then_inc(s["scanned"], 1)
                dve.wait_ge(s["scanned"], n + 1)
                nc.vector.tensor_reduce(A.pos_f[:, slot, :], hot[:, :, :], X, ALU.add).then_inc(s["scanned"], 1)
                n += 2
            dve.wait_ge(s["scanned"], n)
            nc.vector.tensor_copy(A.pos[:, :, :], A.pos_f[:, :, :]).then_inc(s["placed"], 1)


def scatter_rows(nc, c, s, A, rows_dram):
    with nc.Block() as block:
        @block.gpsimd
        def _(pool):
            pool.wait_ge(s["rows_zeroed"], 16 * (TILES // NT))
            for t in range(NT):
                for slot in range(2):
                    nc.gpsimd.indirect_dma_start(
                        out=rows_dram, out_offset=bass.IndirectOffsetOnAxis(ap=A.pos[:, slot, t:t + 1], axis=0),
                        in_=c.h[:, t, :], in_offset=None).then_inc(s["scattered"], 16)
            pool.wait_ge(s["scattered"], 16 * 2 * NT)


def run_routed_experts(nc, c, s, A, rows_dram, out_dram):
    SC, PT, PV, MI = c.SC, c.PT, c.PV, c.MI
    FT = F2 // P
    N_IT = TILES // UNROLL
    U = UNROLL
    rows_v = rows_dram.rearrange("(j p) d -> j p d", p=P)
    out_v = out_dram.rearrange("(j p) d -> j p d", p=P)

    def experts_of(eng, it):
        return [eng.value_load(A.expert[0:1, bass.ds(it * U + r, 1)], min_val=0, max_val=E2 - 1) for r in range(U)]

    with nc.Block() as block:
        @block.sync
        def _(sp):
            with loop(sp, N_IT) as it:
                for r in range(U):
                    sp.wait_ge(s["xs_turned"], it * U + r + 1)
                    sp.dma_start(A.xs[:, r % 2, :], rows_v[bass.ds(it * U + r, 1)].rearrange("o p d -> (o p) d"))\
                        .then_inc(s["xs_even"] if r % 2 == 0 else s["xs_odd"], 16)

        @block.tensor
        def _(pe):
            pe.sem_inc(s["xs_turned"], 2)
            pe.wait_ge(s["weights"], 16 * 5)
            with loop(pe, N_IT) as it:
                expert = experts_of(pe, it)
                j0 = it * U

                def turn_rows(r):
                    pe.wait_ge(s["xs_even"] if r % 2 == 0 else s["xs_odd"], (it * (U // 2) + r // 2 + 1) * 16)
                    pe.wait_ge(s["xt_ready"], j0 + r + 1)
                    nc.tensor.transpose(MI[:, 0:P], A.xs[:, r % 2, :], c.ident[:, :]).then_inc(s["xs_turned"], 1)

                def gate_up(r):
                    pe.wait_ge(s["xt_ready"], j0 + r + 2)
                    pe.wait_ge(s["h_ready"], j0 + r + 1)
                    nc.tensor.matmul(SC[:, 2 * (r % 2), :], A.xt[:, r % 2, :], A.w1[:, bass.ds(expert[r], 1), :].rearrange("p o f -> p (o f)"),
                                     start=True, stop=True)
                    nc.tensor.matmul(SC[:, 2 * (r % 2) + 1, :], A.xt[:, r % 2, :], A.w3[:, bass.ds(expert[r], 1), :].rearrange("p o f -> p (o f)"),
                                     start=True, stop=True).then_inc(s["gu"], 1)

                def turn_hidden(r):
                    pe.wait_ge(s["h_ready"], j0 + r + 3)
                    pe.wait_ge(s["ht_ready"], j0 + r + 1)
                    for f in range(FT):
                        ins_ = nc.tensor.transpose(PT[:, 0, f * P:(f + 1) * P], A.h[:, r % 2, f * P:(f + 1) * P], c.ident[:, :])
                    ins_.then_inc(s["h_turned"], 1)

                def down(r):
                    pe.wait_ge(s["ht_ready"], j0 + r + 2)
                    pe.wait_ge(s["y_normed"], j0 + r + 1)
                    bank = PT[:, 1, 0:D] if r % 2 else PV[:, 0:D]
                    for f in range(FT):
                        ins_ = nc.tensor.matmul(bank, A.ht[:, r % 2, f, :],
                                                A.wd2[:, bass.ds(expert[r] * FT + f, 1), :].rearrange("p o d -> p (o d)"),
                                                start=f == 0, stop=f == FT - 1)
                    ins_.then_inc(s["y_ready"], 1)

                turn_rows(0)
                for r in range(U + 2):
                    if r + 1 < U:
                        turn_rows(r + 1)
                    if r < U:
                        gate_up(r)
                    if 1 <= r <= U:
                        turn_hidden(r - 1)
                    if r >= 2:
                        down(r - 2)

        @block.scalar
        def _(act):
            act.sem_inc(s["xt_ready"], 1)
            act.sem_inc(s["ht_ready"], 1)
            with loop(act, N_IT) as it:
                j0 = it * U

                def copy_rows(r):
                    act.wait_ge(s["xs_turned"], j0 + r + 3)
                    nc.scalar.copy(A.xt[:, r % 2, :], MI[:, 0:P]).then_inc(s["xt_ready"], 1)

                def silu(r):
                    act.wait_ge(s["gu"], j0 + r + 1)
                    act.wait_ge(s["h_ready"], j0 + r + 1)
                    nc.scalar.activation(A.sg[:, r % 2, :], SC[:, 2 * (r % 2), :], ACT.Silu).then_inc(s["silu"], 1)

                def copy_hidden(r):
                    act.wait_ge(s["h_turned"], j0 + r + 1)
                    nc.scalar.copy(A.ht[:, r % 2, :, :], PT[:, 0, :].rearrange("p (f t) -> p f t", f=FT)).then_inc(s["ht_ready"], 1)

                def store(r):
                    act.wait_ge(s["ys_ready"], j0 + r + 3)
                    act.dma_start(out_v[bass.ds(j0 + r, 1)].rearrange("o p d -> (o p) d"), A.ys[:, r % 2, :])\
                        .then_inc(s["ys_even"] if r % 2 == 0 else s["ys_odd"], 16)

                copy_rows(0)
                for r in range(U + 4):
                    if r + 1 < U:
                        copy_rows(r + 1)
                    if r < U:
                        silu(r)
                    if 1 <= r <= U:
                        copy_hidden(r - 1)
                    if r >= 4:
                        store(r - 4)

        @block.vector
        def _(dve):
            dve.sem_inc(s["h_ready"], 2)
            dve.sem_inc(s["y_normed"], 2)
            with loop(dve, N_IT) as it:
                j0 = it * U

                def hidden(r):
                    dve.wait_ge(s["silu"], j0 + r + 1)
                    nc.vector.tensor_tensor(A.h[:, r % 2, :], A.sg[:, r % 2, :], SC[:, 2 * (r % 2) + 1, :], ALU.mult)\
                        .then_inc(s["h_ready"], 1)

                def moments(r):
                    bank = PT[:, 1, 0:D] if r % 2 else PV[:, 0:D]
                    dve.wait_ge(s["y_ready"], j0 + r + 1)
                    dve.nop(nofuse=True)
                    nc.vector.bn_stats(A.yst[:, r % 2, :], bank).then_inc(s["y_stats"], 1)
                    dve.wait_ge(s["y_stats"], j0 + r + 1)
                    dve.nop(nofuse=True)
                    nc.vector.bn_aggr(A.ymv[:, r % 2, :], A.yst[:, r % 2, :]).then_inc(s["y_moments"], 1)

                def normalise(r):
                    bank = PT[:, 1, 0:D] if r % 2 else PV[:, 0:D]
                    dve.wait_ge(s["y_rstd"], j0 + r + 1)
                    nc.vector.tensor_scalar(A.yn[:, r % 2, :], bank, A.ymv[:, r % 2, 0:1], A.yrstd[:, r % 2:r % 2 + 1],
                                            ALU.subtract, ALU.mult).then_inc(s["y_normed"], 1)

                for r in range(U + 2):
                    if r >= 2:
                        moments(r - 2)
                    if r < U:
                        hidden(r)
                    if r >= 2:
                        normalise(r - 2)

        @block.gpsimd
        def _(pool):
            pool.sem_inc(s["ys_ready"], 2)
            pool.sem_inc(s["ys_even"], 16)
            pool.sem_inc(s["ys_odd"], 16)
            pool.wait_ge(s["weights"], 16 * 5)
            with loop(pool, N_IT) as it:
                expert = experts_of(pool, it)
                j0 = it * U
                for r in range(U):
                    pool.wait_ge(s["y_moments"], j0 + r + 1)
                    pool.nop(nofuse=True)
                    nc.gpsimd.tensor_scalar(A.yvar[:, :], A.ymv[:, r % 2, 1:2], EPS, None, ALU.add).then_inc(s["y_vare"], 1)
                    pool.wait_ge(s["y_vare"], j0 + r + 1)
                    nc.gpsimd.tensor_tensor(A.yrstd[:, r % 2:r % 2 + 1], A.yvar[:, :], c.mhalf[:, 0:1], ALU.pow).then_inc(s["y_rstd"], 1)
                    pool.wait_ge(s["y_normed"], j0 + r + 3)
                    nc.gpsimd.tensor_tensor(A.yg[:, :], A.yn[:, r % 2, :],
                                            A.gamma[:, bass.ds(expert[r], 1), :].rearrange("p o d -> p (o d)"), ALU.mult).then_inc(s["y_scaled"], 1)
                    pool.wait_ge(s["y_scaled"], j0 + r + 1)
                    pool.wait_ge(s["ys_even"] if r % 2 == 0 else s["ys_odd"], (it * (U // 2) + r // 2 + 1) * 16)
                    nc.gpsimd.tensor_tensor(A.ys[:, r % 2, :], A.yg[:, :],
                                            A.beta[:, bass.ds(expert[r], 1), :].rearrange("p o d -> p (o d)"), ALU.add).then_inc(s["ys_ready"], 1)


def gather_and_add(nc, c, s, A, out_dram, y1, y2):
    with nc.Block() as block:
        @block.gpsimd
        def _(pool):
            pool.wait_ge(s["ys_even"], 16 + 16 * TILES // 2)
            pool.wait_ge(s["ys_odd"], 16 + 16 * TILES // 2)
            for t in range(NT):
                for slot, y in enumerate((y1, y2)):
                    nc.gpsimd.indirect_dma_start(
                        out=y[:, t, :], out_offset=None, in_=out_dram,
                        in_offset=bass.IndirectOffsetOnAxis(ap=A.pos[:, slot, t:t + 1], axis=0)).then_inc(s[GATHERED[t // TP]], 16)

        @block.vector
        def _(dve):
            for g, gathered in enumerate(GATHERED):
                dve.wait_ge(s[gathered], 16 * 2 * TP)
                for slot, (y, w) in enumerate(((y1, A.w1), (y2, A.w2))):
                    for t in range(g * TP, g * TP + TP):
                        if slot == 1 and t == g * TP:
                            dve.wait_ge(s["y_added"], g * 2 * TP + TP)
                        nc.vector.scalar_tensor_tensor(c.x[:, t, :], y[:, t, :], w[:, t:t + 1], c.x[:, t, :], ALU.mult, ALU.add)\
                            .then_inc(s["y_added"], 1)


def routed_ffn(nc, c, a, W):
    rows_dram = nc.dram_tensor("routed_rows", (TILES * P, D), F32, kind="Internal").ap()
    out_dram = nc.dram_tensor("routed_out", (TILES * P, D), F32, kind="Internal").ap()
    with ExitStack() as scope:
        def sb(name, shape, dt=F32):
            return scope.enter_context(nc.sbuf_tensor(f"F2_{name}", shape, dt))
        s = stage_sems(nc, scope, "F2", GATE_SEMS + ROUTE_SEMS + PLACE_SEMS + GATHERED + ["xs_even", "xs_odd", "ys_even", "ys_odd"])
        scope.callback(clear_sems, nc, s)
        A = Parts()
        A.prob = sb("prob", [P, NT, E2])
        A.hot1 = sb("hot1", [P, NT, E2])
        A.hot2 = sb("hot2", [P, NT, E2])
        A.rest = sb("rest", [P, NT, E2])
        A.logits = sb("logits", [P, NT, E2])
        A.r1 = sb("r1", [P, NT])
        A.r2 = sb("r2", [P, NT])
        A.r3 = sb("r3", [P, NT])
        A.r4 = sb("r4", [P, NT])
        A.w1 = sb("weight1", [P, NT])
        A.w2 = sb("weight2", [P, NT])
        A.pos = sb("pos", [P, 2, NT], I32)
        A.expert = sb("expert", [P, TILES], I32)
        with ExitStack() as inner:
            def sbi(name, shape, dt=F32):
                return inner.enter_context(nc.sbuf_tensor(f"F2_{name}", shape, dt))
            K = Parts()
            K.w1 = sbi("w1", [P, E2, F2])
            K.w3 = sbi("w3", [P, E2, F2])
            K.wd2 = sbi("w2", [P, E2 * F2 // P, D])
            K.gamma = sbi("gamma", [P, E2, D])
            K.beta = sbi("beta", [P, E2, D])
            with nc.Block() as block:
                @block.sync
                def _(sp):
                    sp.wait_ge(s["rows_zeroed"], 16 * (TILES // NT))
                    for t, n in ((K.w1, "F2_w1"), (K.w3, "F2_w3"), (K.wd2, "F2_w2")):
                        sp.dma_start(t[:, :, :], a[n]).then_inc(s["weights"], 16)
                    for t, n in ((K.gamma, "F2_gamma"), (K.beta, "F2_beta")):
                        sp.dma_start(t[:, :, :].rearrange("p e d -> p (e d)"), a[n].partition_broadcast(P)).then_inc(s["weights"], 16)

                @block.vector
                def _(dve):
                    nc.vector.memset(c.h[:, :, :], 0.0).then_inc(s["consts0"], 1)

                @block.scalar
                def _(act):
                    act.wait_ge(s["consts0"], 1)
                    for q in range(TILES // NT):
                        act.dma_start(rows_dram[q * NT * P:(q + 1) * NT * P, :].rearrange("(p t) d -> p (t d)", t=NT),
                                      c.h[:, :, :].rearrange("p t d -> p (t d)")).then_inc(s["rows_zeroed"], 16)
                    act.wait_ge(s["rows_zeroed"], 16 * (TILES // NT))
            with ExitStack() as early:
                def sbe(name, shape, dt=F32):
                    return early.enter_context(nc.sbuf_tensor(f"F2_{name}", shape, dt))
                A.st, A.mv = sbe("st", [P, NT, 6]), sbe("mv", [P, NT, 2])
                A.vare, A.rstd = sbe("vare", [P, NT]), sbe("rstd", [P, NT])
                xnt = sbe("xnt", [P, B * S])
                gate_tokens(nc, c, s, A, "ln", c.x, c.h, xnt, W.gate[:, :], None, E2, W.loaded, W.n_loaded, W.bias[:, :])
                choose_experts(nc, c, s, A, E2, False)
            with ExitStack() as early:
                def sbe(name, shape, dt=F32):
                    return early.enter_context(nc.sbuf_tensor(f"F2_{name}", shape, dt))
                A.tri, A.ones_bf, A.both = sbe("tri", [P, P], BF16), sbe("ones_bf", [P, P], BF16), sbe("both", [P, NT, E2], BF16)
                A.base, A.totals = sbe("base", [P, NT + 1, E2]), sbe("totals", [P, NT, E2])
                A.need, A.start = sbe("need", [P, E2]), sbe("start", [P, E2 + 1])
                A.ended, A.expert_f, A.pos_f = sbe("ended", [P, TILES, E2]), sbe("expert_f", [P, TILES]), sbe("pos_f", [P, 2, NT])
                place_rows(nc, c, s, A)
            scatter_rows(nc, c, s, A, rows_dram)
            K.expert = A.expert
            K.xs, K.xt = sbi("xs", [P, 2, D]), sbi("xt", [P, 2, P])
            K.sg, K.h, K.ht = sbi("sg", [P, 2, F2]), sbi("h", [P, 2, F2]), sbi("ht", [P, 2, F2 // P, P])
            K.yst, K.ymv, K.yvar, K.yrstd = sbi("yst", [P, 2, 6]), sbi("ymv", [P, 2, 2]), sbi("yvar", [P, 1]), sbi("yrstd", [P, 2])
            K.yn, K.yg, K.ys = sbi("yn", [P, 2, D]), sbi("yg", [P, D]), sbi("ys", [P, 2, D])
            run_routed_experts(nc, c, s, K, rows_dram, out_dram)
        y2 = sb("y2", [P, NT, D])
        gather_and_add(nc, c, s, A, out_dram, c.h, y2)


QUANT_SEMS = """partial moments variance rstd normed chain w_quantised w_turned wt_ready pmax pmax_turned gmax gmax_spread
    scale_ready rounded xq_ready xq_turned up_clipped up_ready
    xqt_ready projected copied sigmoid_in sigmoid o_ready down added loaded""".split()
I3 = 384
IT3 = I3 // P
BLOCK = 32
QMAX = 32767.0
SCALE_MIN = 1e-12


def quantised_ffn(nc, c, a):
    SC, PT, PV, MI = c.SC, c.PT, c.PV, c.MI
    N = B * S
    XS, US, GS, GG, OS = range(5)
    with ExitStack() as scope:
        def sb(name, shape, dt=F32):
            return scope.enter_context(nc.sbuf_tensor(f"F3_{name}", shape, dt))
        s = stage_sems(nc, scope, "F3", QUANT_SEMS)
        scope.callback(clear_sems, nc, s)
        st, mv = sb("ln_stats", [P, NT, 6]), sb("ln_moments", [P, NT, 2])
        vare, rstd = sb("ln_variance", [P, NT]), sb("ln_rstd", [P, NT])
        w = sb("w", [P, 3, I3])
        wm, ws, wi = sb("wm", [P, 3 * I3 // BLOCK]), sb("ws", [P, 3 * I3 // BLOCK]), sb("wi", [P, 3 * I3 // BLOCK])
        wt = sb("wt", [P, 3, I3])
        xq, xqt = sb("xq", [P, NT, D]), sb("xqt", [P, N])
        up, gate, sig = sb("up", [P, IT3, N]), sb("gate", [P, IT3, N]), sb("sig", [P, IT3, N])
        pm, gm = sb("pm", [P, 5 * IT3]), sb("gm", [1, 5])
        sc, inv, magic = sb("sc", [P, 5]), sb("inv", [P, 5]), sb("magic", [P, 1])
        block = scope.enter_context(nc.Block())

        @block.gpsimd
        def _(pool):
            pool.wait_ge(s["moments"], NT)
            nc.gpsimd.tensor_scalar(vare[:, :], mv[:, :, 1], EPS, None, ALU.add).then_inc(s["variance"], 1)
            pool.wait_ge(s["variance"], 1)
            nc.gpsimd.tensor_tensor(rstd[:, :], vare[:, :], c.mhalf[:, 0:NT], ALU.pow).then_inc(s["rstd"], 1)
            for t in range(IT3 - 1):
                pool.wait_ge(s["rounded"], 1 + t + 1)
                nc.gpsimd.tensor_scalar(up[:, t, :], up[:, t, :], MAGIC, -QMAX - 1.0, ALU.subtract, ALU.max).then_inc(s["up_clipped"], 1)
                pool.wait_ge(s["up_clipped"], t + 1)
                nc.gpsimd.tensor_scalar(up[:, t, :], up[:, t, :], QMAX, sc[:, US:US + 1], ALU.min, ALU.mult).then_inc(s["up_ready"], 1)

        @block.sync
        def _(sp):
            sp.dma_start(w[:, :, :], a["F3_w"]).then_inc(s["loaded"], 16)

        @block.vector
        def _(dve):
            links = [0]

            def link(ins_):
                links[0] += 1
                ins_.then_inc(s["chain"], 1)
                dve.wait_ge(s["chain"], links[0])

            def scale_of(q):
                dve.wait_ge(s["pmax_turned"], q + 1)
                nc.vector.tensor_reduce(gm[0:1, q:q + 1], MI[0:1, 0:P], X, ALU.max).then_inc(s["gmax"], 1)
                dve.wait_ge(s["gmax_spread"], q + 1)
                link(nc.vector.tensor_scalar(sc[:, q:q + 1], PV[:, q:q + 1], 1.0 / QMAX, SCALE_MIN, ALU.mult, ALU.max))
                nc.vector.reciprocal(inv[:, q:q + 1], sc[:, q:q + 1]).then_inc(s["scale_ready"], 1)

            def tile_max(q, srcs, ready):
                for t, src in enumerate(srcs):
                    if ready is not None:
                        dve.wait_ge(ready[0], ready[1] + t * ready[2])
                    ins_ = nc.vector.tensor_reduce(pm[:, 3 * q + t:3 * q + t + 1], src, X, ALU.max, apply_absolute_value=True)
                    if len(srcs) == 1:
                        ins_.then_inc(s["pmax"], 1)
                    else:
                        link(ins_)
                if len(srcs) > 1:
                    nc.vector.tensor_reduce(pm[:, 3 * q:3 * q + 1], pm[:, 3 * q:3 * q + 3], X, ALU.max).then_inc(s["pmax"], 1)

            def quantise(q, t, ap):
                link(nc.vector.tensor_scalar(ap, ap, MAGIC, -QMAX - 1.0, ALU.subtract, ALU.max))
                link(nc.vector.tensor_scalar(ap, ap, QMAX, sc[:, q:q + 1], ALU.min, ALU.mult))

            link(nc.vector.memset(magic[:, :], MAGIC))
            for t in range(NT):
                nc.vector.bn_stats(st[:, t, :], c.x[:, t, :]).then_inc(s["partial"], 1)
            dve.wait_ge(s["partial"], NT)
            for t in range(NT):
                nc.vector.bn_aggr(mv[:, t, :], st[:, t, :]).then_inc(s["moments"], 1)
            dve.wait_ge(s["rstd"], 1)
            for t in range(NT):
                nc.vector.tensor_scalar(xq[:, t, :], c.x[:, t, :], mv[:, t, 0:1], rstd[:, t:t + 1], ALU.subtract, ALU.mult)\
                    .then_inc(s["normed"], 1)
            dve.wait_ge(s["normed"], NT)
            xf = xq[:, :, :].rearrange("p t d -> p (t d)")
            tile_max(XS, [xf], None)
            dve.wait_ge(s["loaded"], 16)
            wb = w[:, :, :].rearrange("p a (b k) -> p (a b) k", k=BLOCK)

            def bc(t):
                return t[:, :].unsqueeze(2).to_broadcast([P, 3 * I3 // BLOCK, BLOCK])
            link(nc.vector.tensor_reduce(wm[:, :], wb, X, ALU.max, apply_absolute_value=True))
            link(nc.vector.tensor_scalar(ws[:, :], wm[:, :], 1.0 / 7.0, SCALE_MIN, ALU.mult, ALU.max))
            link(nc.vector.reciprocal(wi[:, :], ws[:, :]))
            link(nc.vector.tensor_tensor(wb, wb, bc(wi), ALU.mult))
            link(nc.vector.tensor_scalar(wb, wb, MAGIC, None, ALU.add))
            link(nc.vector.tensor_scalar(wb, wb, MAGIC, -8.0, ALU.subtract, ALU.max))
            link(nc.vector.tensor_scalar(wb, wb, 7.0, None, ALU.min))
            nc.vector.tensor_tensor(wb, wb, bc(ws), ALU.mult).then_inc(s["w_quantised"], 1)
            scale_of(XS)
            dve.wait_ge(s["rounded"], 1)
            link(nc.vector.tensor_scalar(xf, xf, MAGIC, -QMAX - 1.0, ALU.subtract, ALU.max))
            nc.vector.tensor_scalar(xf, xf, QMAX, sc[:, XS:XS + 1], ALU.min, ALU.mult).then_inc(s["xq_ready"], 1)
            for q, (k, tens) in ((US, (0, up)), (GS, (1, gate))):
                tile_max(q, [tens[:, t, :] for t in range(IT3)], (s["copied"], (k * IT3 + 1) * 4, 4))
                scale_of(q)
            for t in range(IT3):
                dve.wait_ge(s["rounded"], 1 + IT3 + t + 1)
                link(nc.vector.tensor_scalar(gate[:, t, :], gate[:, t, :], MAGIC, -QMAX - 1.0, ALU.subtract, ALU.max))
                nc.vector.tensor_scalar(gate[:, t, :], gate[:, t, :], QMAX, sc[:, GS:GS + 1], ALU.min, ALU.mult)\
                    .then_inc(s["sigmoid_in"], 1)
            dve.wait_ge(s["rounded"], 1 + IT3)
            quantise(US, IT3 - 1, up[:, IT3 - 1, :])
            for t in range(IT3):
                dve.wait_ge(s["sigmoid"], 2 * t + 2)
                link(nc.vector.tensor_scalar(sig[:, t, :], sig[:, t, :], MAGIC, 65535.0, ALU.subtract, ALU.min))
                link(nc.vector.scalar_tensor_tensor(gate[:, t, :], sig[:, t, :], 1.0 / 65536.0, gate[:, t, :], ALU.mult, ALU.mult))
            tile_max(GG, [gate[:, t, :] for t in range(IT3)], None)
            scale_of(GG)
            for t in range(IT3):
                dve.wait_ge(s["rounded"], 1 + 2 * IT3 + t + 1)
                quantise(GG, t, gate[:, t, :])
                if t < IT3 - 1:
                    dve.wait_ge(s["up_ready"], t + 1)
                link(nc.vector.tensor_tensor(gate[:, t, :], gate[:, t, :], up[:, t, :], ALU.mult))
            tile_max(OS, [gate[:, t, :] for t in range(IT3)], None)
            scale_of(OS)
            for t in range(IT3):
                dve.wait_ge(s["rounded"], 1 + 3 * IT3 + t + 1)
                link(nc.vector.tensor_scalar(gate[:, t, :], gate[:, t, :], MAGIC, -QMAX - 1.0, ALU.subtract, ALU.max))
                nc.vector.tensor_scalar(gate[:, t, :], gate[:, t, :], QMAX, sc[:, OS:OS + 1], ALU.min, ALU.mult)\
                    .then_inc(s["o_ready"], 1)
            for q in range(NT // TP):
                dve.wait_ge(s["down"], q + 1)
                xt = c.x[:, q * TP:(q + 1) * TP, :].rearrange("p t d -> p (t d)")
                nc.vector.tensor_tensor(xt, xt, SC[:, q, :], ALU.add).then_inc(s["added"], 1)

        @block.scalar
        def _(act):
            def rounded(q, dst, src, n_scale):
                act.wait_ge(s["scale_ready"], n_scale)
                nc.scalar.activation(dst, src, ACT.Identity, bias=magic[:, 0:1], scale=inv[:, q:q + 1]).then_inc(s["rounded"], 1)

            xf = xq[:, :, :].rearrange("p t d -> p (t d)")
            rounded(XS, xf, xf, 1)
            for k in range(3):
                act.wait_ge(s["w_turned"], k + 1)
                nc.scalar.copy(wt[:, k, :], PT[:, k % 2, 0:I3]).then_inc(s["wt_ready"], 1)
            for ch in range(4):
                act.wait_ge(s["xq_turned"], ch + 1)
                nc.scalar.copy(xqt[:, ch * PAIR:(ch + 1) * PAIR], SC[:, ch, :]).then_inc(s["xqt_ready"], 1)
            for k, tens in enumerate((up, gate)):
                for t in range(IT3):
                    for ch in range(4):
                        act.wait_ge(s["projected"], (k * IT3 + t) * 4 + ch + 1)
                        nc.scalar.copy(tens[:, t, ch * PAIR:(ch + 1) * PAIR], SC[:, ch, :]).then_inc(s["copied"], 1)
            for q, tens, n_scale in ((US, up, 2), (GS, gate, 3)):
                for t in range(IT3):
                    rounded(q, tens[:, t, :], tens[:, t, :], n_scale)
            for t in range(IT3):
                act.wait_ge(s["sigmoid_in"], t + 1)
                nc.scalar.activation(sig[:, t, :], gate[:, t, :], ACT.Sigmoid).then_inc(s["sigmoid"], 1)
                act.wait_ge(s["sigmoid"], 2 * t + 1)
                nc.scalar.activation(sig[:, t, :], sig[:, t, :], ACT.Identity, bias=magic[:, 0:1], scale=65536.0).then_inc(s["sigmoid"], 1)
            for q, n_scale in ((GG, 4), (OS, 5)):
                for t in range(IT3):
                    rounded(q, gate[:, t, :], gate[:, t, :], n_scale)

        @block.tensor
        def _(pe):
            def spread_max(q):
                pe.wait_ge(s["pmax"], q + 1)
                nc.tensor.transpose(MI[0:1, 0:P], pm[:, 3 * q:3 * q + 1], c.ident[:, :]).then_inc(s["pmax_turned"], 1)
                pe.wait_ge(s["gmax"], q + 1)
                nc.tensor.matmul(PV[:, q:q + 1], c.ones_row[:, :], gm[0:1, q:q + 1], start=True, stop=True).then_inc(s["gmax_spread"], 1)

            spread_max(XS)
            pe.wait_ge(s["w_quantised"], 1)
            for k in range(3):
                if k == 2:
                    pe.wait_ge(s["wt_ready"], 1)
                for t in range(IT3):
                    ins_ = nc.tensor.transpose(PT[:, k % 2, t * P:(t + 1) * P], w[:, k, t * P:(t + 1) * P], c.ident[:, :])
                ins_.then_inc(s["w_turned"], 1)
            pe.wait_ge(s["xq_ready"], 1)
            for ch in range(4):
                for tt in range(TP):
                    ins_ = nc.tensor.transpose(SC[:, ch, tt * P:(tt + 1) * P], xq[:, ch * TP + tt, :], c.ident[:, :])
                ins_.then_inc(s["xq_turned"], 1)
            pe.wait_ge(s["wt_ready"], 3)
            pe.wait_ge(s["xqt_ready"], 4)
            for k in range(2):
                for t in range(IT3):
                    for ch in range(4):
                        n = (k * IT3 + t) * 4 + ch
                        if n >= 4:
                            pe.wait_ge(s["copied"], n - 3)
                        nc.tensor.matmul(SC[:, ch, :], wt[:, k, t * P:(t + 1) * P], xqt[:, ch * PAIR:(ch + 1) * PAIR],
                                         start=True, stop=True).then_inc(s["projected"], 1)
                if k == 1:
                    spread_max(US)
            spread_max(GS)
            spread_max(GG)
            spread_max(OS)
            pe.wait_ge(s["o_ready"], IT3)
            for q in range(NT // TP):
                for tt in range(TP):
                    tok = (q * TP + tt) * P
                    for t in range(IT3):
                        ins_ = nc.tensor.matmul(SC[:, q, tt * D:(tt + 1) * D], gate[:, t, tok:tok + P], wt[:, 2, t * P:(t + 1) * P],
                                                start=t == 0, stop=t == IT3 - 1)
                ins_.then_inc(s["down"], 1)


def build(nc, a, out):
    with ExitStack() as top:
        def sb(name, shape, dt=F32):
            return top.enter_context(nc.sbuf_tensor(name, shape, dt))

        def sem(name):
            return top.enter_context(nc.semaphore(name))

        c = Parts()
        c.x = sb("x", [P, NT, D])
        c.ctx = sb("ctx_t", [P, B * S])
        c.ident = sb("ident", [P, P])
        c.mhalf = sb("mhalf", [P, NT])
        c.ones_row = sb("ones_row", [1, P])
        c.ones_mat = sb("ones_mat", [P, P])
        c.slope_ident = sb("slope_ident", [P, H, P], BF16)
        c.h = sb("h", [P, NT, D])
        c.order = sb("order", [P, 16])
        c.count = sb("count", [P, TILES])
        c.const_ready = sem("const_ready")
        c.ctx_loaded = sem("ctx_loaded")
        c.SC = top.enter_context(nc.psum_tensor("SC", [P, 4, 512], F32))
        c.PT = top.enter_context(nc.psum_tensor("PT", [P, 2, 512], F32))
        c.PV = top.enter_context(nc.psum_tensor("PV", [P, 512], F32))
        c.MI = top.enter_context(nc.psum_tensor("MI", [P, 512], F32))
        x_loaded, out_stored, zeroed = sem("x_loaded"), sem("out_stored"), sem("zeroed")
        W = []
        for l in range(4):
            w = Parts()
            w.wq = sb(f"X{l}_wq", [P, G, P])
            w.wk = sb(f"X{l}_wk", [P, G, P])
            w.wv = sb(f"X{l}_wv", [P, D])
            w.wo = sb(f"X{l}_wo", [P, 1, D])
            w.bq = sb(f"X{l}_bq", [P, G])
            w.bk = sb(f"X{l}_bk", [P, G])
            w.brow = sb(f"X{l}_brow", [P, 2, D])
            w.bias = sb(f"X{l}_bias", [P, 2, S]) if l != 3 else None
            w.mask_i = sb(f"X{l}_mask", [P, 2, S], I32) if l in (0, 3) else None
            w.maskt_i = sb(f"X{l}_maskt", [P, 2, S], I32) if l == 0 else None
            w.loaded = sem(f"X{l}_loaded")
            w.n_loaded = 0
            W.append(w)

        F0 = Parts()
        F0.gate = sb("F0_gate_w", [P, 8])
        F0.loaded = sem("F0_loaded")
        F0.n_loaded = 16
        F1 = Parts()
        F1.gate = sb("F1_gate_w", [P, 8])
        F1.w_ln = sb("F1_w_ln", [P, 1])
        F1.bias = sb("F1_bias", [1, 8])
        F1.loaded = sem("F1_loaded")
        F1.n_loaded = 64
        F2w = Parts()
        F2w.gate = sb("F2_gate_w", [P, E2])
        F2w.bias = sb("F2_bias", [1, E2])
        F2w.loaded = sem("F2_loaded")
        F2w.n_loaded = 48
        latent_scope = top.enter_context(ExitStack())

        def sbm(name, shape, dt=F32):
            return latent_scope.enter_context(nc.sbuf_tensor(name, shape, dt))

        M = Parts()
        M.wq = sbm("M_wq", [P, 8, P])
        M.wqs = sbm("M_wqs", [P, 8, P])
        M.wkr = sbm("M_wkr", [P, P])
        M.wks = sbm("M_wks", [P, P])
        M.wlat = sbm("M_wlat", [P, P])
        M.wkb = sbm("M_wkb", [P, 8, P])
        M.wvb = sbm("M_wvb", [P, 4 * P])
        M.wo = sbm("M_wo", [P, 4, D])
        M.rope_q = sbm("M_rope_q", [P, 2, PAIR])
        M.rope_k = sbm("M_rope_k", [P, 2, PAIR])
        M.bias = sbm("M_bias", [P, 2, S])
        M.w_ln = sbm("M_w_ln", [P, 1])
        M.loaded = sem("M_loaded")
        M.n_loaded = 12 * 16

        def load_cross(sp, l, w):
            for n, t in (("wq", w.wq), ("wk", w.wk), ("wv", w.wv), ("wo", w.wo), ("bq", w.bq), ("bk", w.bk),
                         ("bias", w.bias), ("mask", w.mask_i), ("maskt", w.maskt_i)):
                if t is not None:
                    sp.dma_start(t[tuple(slice(None) for _ in t.shape)], a[f"X{l}_{n}"]).then_inc(w.loaded, 16)
                    w.n_loaded += 16
            sp.dma_start(w.brow[:, :, :].rearrange("p k d -> p (k d)"), a[f"X{l}_brow"].partition_broadcast(P)).then_inc(w.loaded, 16)
            w.n_loaded += 16

        def load_later_stages(sp):
            sp.dma_start(F0.gate[:, :], a["F0_gate"]).then_inc(F0.loaded, 16)
            load_cross(sp, 1, W[1])
            for n, t in (("wq", M.wq), ("wqs", M.wqs), ("wkr", M.wkr), ("wks", M.wks), ("wlat", M.wlat), ("wkb", M.wkb),
                         ("wvb", M.wvb), ("wo", M.wo), ("rope_q", M.rope_q), ("rope_k", M.rope_k), ("bias", M.bias),
                         ("w_ln", M.w_ln)):
                sp.dma_start(t[tuple(slice(None) for _ in t.shape)], a[f"M_{n}"]).then_inc(M.loaded, 16)
            sp.dma_start(F1.gate[:, :], a["F1_gate"]).then_inc(F1.loaded, 16)
            sp.dma_start(F1.w_ln[:, :], a["F1_w_ln"]).then_inc(F1.loaded, 16)
            sp.dma_start(F1.bias[:, :], a["F1_bias"]).then_inc(F1.loaded, 16)
            sp.dma_start(c.order[:, :], a["order"]).then_inc(F1.loaded, 16)
            load_cross(sp, 2, W[2])
            sp.dma_start(F2w.gate[:, :], a["F2_gate"]).then_inc(F2w.loaded, 16)
            sp.dma_start(F2w.bias[:, :], a["F2_bias"]).then_inc(F2w.loaded, 16)
            sp.dma_start(c.count[:, :], a["count"]).then_inc(F2w.loaded, 16)
            load_cross(sp, 3, W[3])

        with nc.Block() as block:
            @block.sync
            def _(sp):
                sp.dma_start(c.x[:, :, :], a["x"]).then_inc(x_loaded, 16)
                sp.dma_start(c.ctx[:, :], a["ctx"]).then_inc(c.ctx_loaded, 16)
                load_cross(sp, 0, W[0])
                sp.wait_ge(x_loaded, 16)

            @block.gpsimd
            def _(pool):
                nc.gpsimd.memset(c.ident[:, :], 0.0).then_inc(zeroed, 1)
                nc.gpsimd.memset(c.slope_ident[:, :, :], 0.0).then_inc(zeroed, 1)
                nc.gpsimd.memset(c.ones_mat[:, :], 1.0).then_inc(c.const_ready, 1)
                nc.gpsimd.memset(c.ones_row[:, :], 1.0)
                nc.gpsimd.memset(c.mhalf[:, :], -0.5).then_inc(c.const_ready, 1)
                pool.wait_ge(zeroed, 2)
                nc.gpsimd.affine_select(out=c.ident[:, :], in_=c.ident[:, :], compare_op=ALU.not_equal, fill=1.0, base=0,
                                        pattern=[[-1, P]], channel_multiplier=1).then_inc(c.const_ready, 1)
                for h in range(H):
                    ins_ = nc.gpsimd.affine_select(out=c.slope_ident[:, h, :], in_=c.slope_ident[:, h, :],
                                                   compare_op=ALU.not_equal, fill=2.0 ** -(h + 1), base=0,
                                                   pattern=[[-1, P]], channel_multiplier=1)
                ins_.then_inc(c.const_ready, 1)

        attention(nc, c, W[0], "A0", "alibi", load_later_stages)
        expert_choice_ffn(nc, c, a, F0)
        attention(nc, c, W[1], "A1", "add")
        attention(nc, c, M, "AM", "mla")
        latent_scope.close()
        shared_and_routed_ffn(nc, c, a, F1)
        attention(nc, c, W[2], "A2", "add")
        routed_ffn(nc, c, a, F2w)
        attention(nc, c, W[3], "A3", "mul")
        quantised_ffn(nc, c, a)

        with nc.Block() as block:
            @block.sync
            def _(sp):
                for w in W + [F0, F1, F2w]:
                    sp.wait_ge(w.loaded, w.n_loaded)
                sp.dma_start(out, c.x[:, :, :]).then_inc(out_stored, 16)
                sp.wait_ge(out_stored, 16)




def lay_out(i):
    import numpy as np

    def tiles(x):
        return np.ascontiguousarray(x.reshape(x.shape[0] // P, P, *x.shape[1:]).swapaxes(0, 1))

    def slots(w):
        o = np.zeros((w.shape[0], G, HG, 32), w.dtype)
        o[:, :, :, 0:HD] = w.reshape(w.shape[0], G, HG, HD)
        return o.reshape(w.shape[0], G, P)

    a = {"x": tiles(i["x"].reshape(B * S, D)), "ctx": np.ascontiguousarray(i["ctx_1024"].reshape(B * S, D).T)}
    zero = np.zeros(D, np.float32)
    layers = [
        (i["L0_xattn_wq_w"].T, i["L0_xattn_wk_w"].T, i["L0_xattn_wv_w"].T, i["L0_xattn_out_w"].T,
         i["L0_xattn_wq_b"], i["L0_xattn_wk_b"], i["L0_xattn_wv_b"], i["L0_xattn_out_b"]),
        (i["L1_xattn_wq"].reshape(D, D), i["L1_xattn_wk"].reshape(D, D), i["L1_xattn_wv"].reshape(D, D),
         i["L1_xattn_wo"].reshape(D, D), zero, zero, zero, zero),
        (i["L2_xattn_Wq"], i["L2_xattn_Wk"], i["L2_xattn_Wv"], i["L2_xattn_Wo"],
         i["L2_xattn_bq"], i["L2_xattn_bk"], i["L2_xattn_bv"], i["L2_xattn_bo"]),
        (i["L3_xattn_wq_w"].T, i["L3_xattn_wk_w"].T, i["L3_xattn_wv_w"].T, i["L3_xattn_wo_w"].T,
         i["L3_xattn_wq_b"], i["L3_xattn_wk_b"], i["L3_xattn_wv_b"], i["L3_xattn_wo_b"]),
    ]
    for l, (wq, wk, wv, wo, bq, bk, bv, bo) in enumerate(layers):
        a[f"X{l}_wq"], a[f"X{l}_wk"] = slots(wq), slots(wk)
        a[f"X{l}_wv"], a[f"X{l}_wo"] = np.ascontiguousarray(wv), np.ascontiguousarray(wo)[:, None]
        sq, sk = slots(bq[None])[0], slots(bk[None])[0]
        if l == 3:
            sq.reshape(G, HG, 32)[:, :, HD] = 1.0
            sk.reshape(G, HG, 32)[:, :, HD] = -1e-9 * HD ** 0.5
        a[f"X{l}_bq"], a[f"X{l}_bk"] = np.ascontiguousarray(sq.T), np.ascontiguousarray(sk.T)
        a[f"X{l}_brow"] = np.concatenate([bv, bo])
    pos = np.arange(S)
    a["X0_bias"] = tiles(-np.maximum(pos[:, None] - pos[None, :], 0).astype(np.float32))
    a["X0_mask"] = tiles(i["mask_1x1xSxS2_ik0"].reshape(S, S))
    a["X0_maskt"] = tiles(np.ascontiguousarray(i["mask_1x1xSxS2_ik0"].reshape(S, S).T))
    a["X1_bias"] = tiles(i["fside_1x1xSxS2_0"].reshape(S, S))
    a["X2_bias"] = tiles(i["mask_1x1xSxS2_fk0"].reshape(S, S))
    a["X3_mask"] = tiles(i["mask_1x1xSxS2_ik1"].reshape(S, S))
    wg, wu, wd = (i[f"L0_ffn_{n}"] for n in ("Wg", "Wu", "Wd"))
    a["F0_gate"] = i["L0_ffn_gate_w"]
    a["F0_wg"], a["F0_wu"] = wg.reshape(8, D, 2, P), wu.reshape(8, D, 2, P)
    a["F0_wd"] = np.ascontiguousarray(wd.reshape(8, 2, P, D).swapaxes(1, 2))
    wg, wu, wd = (i[f"L1_ffn_{n}"] for n in ("Wg", "Wu", "Wd"))
    sg, su, sd = (i[f"L1_ffn_{n}"] for n in ("sWg", "sWu", "sWd"))
    a["F1_gate"], a["F1_w_ln"], a["F1_bias"] = i["L1_ffn_Wgate"], i["L1_ffn_w_ln2"][:, None], i["L1_ffn_expert_bias"][None]

    def side_by_side(w, sw):
        w = np.concatenate([w, sw, np.zeros_like(sw)])
        return np.ascontiguousarray(w.reshape(5, 2, D, 64).transpose(0, 2, 1, 3).reshape(5, D, 1, P))

    a["F1_wg"], a["F1_wu"] = side_by_side(wg, sg), side_by_side(wu, su)
    a["F1_wd"] = np.concatenate([wd, sd, np.zeros_like(sd)]).reshape(5, P, 1, D)

    a["F2_gate"], a["F2_bias"] = i["L2_ffn_Wr"], i["L2_ffn_br"][None]
    a["F2_w1"], a["F2_w3"] = (np.ascontiguousarray(i[f"L2_ffn_{n}"].swapaxes(0, 1)) for n in ("W1", "W3"))
    a["F2_w2"] = np.ascontiguousarray(i["L2_ffn_W2"].reshape(E2 * F2 // P, P, D).swapaxes(0, 1))
    a["F2_gamma"], a["F2_beta"] = i["L2_ffn_gamma"].reshape(-1), i["L2_ffn_beta"].reshape(-1)
    a["count"] = np.tile(np.arange(TILES, dtype=np.float32), (P, 1))

    a["F3_w"] = np.stack([tiles(i["L3_ffn_w_up"]).reshape(P, I3), tiles(i["L3_ffn_w_gate"]).reshape(P, I3),
                          i["L3_ffn_w_down"]], 1)

    wq, wkva, wkvb = i["L1_ffn_Wq"], i["L1_ffn_Wkva"], i["L1_ffn_Wkvb"]
    swap = np.arange(32) ^ 1
    wq_h = wq.reshape(D, H, 2, 32)
    a["M_wq"] = wq.reshape(D, 8, P)
    a["M_wqs"] = np.concatenate([wq_h[:, :, 0:1], wq_h[:, :, 1:2, swap]], 2).reshape(D, 8, P)
    for n, cols in (("M_wkr", wkva[:, 16:48]), ("M_wks", wkva[:, 16:48][:, swap])):
        a[n] = np.zeros((D, 2, 2, 32), np.float32)
        a[n][:, :, 1] = cols[:, None]
        a[n] = a[n].reshape(D, P)
    a["M_wlat"] = np.zeros((D, P), np.float32)
    a["M_wlat"][:, 0:16] = wkva[:, 0:16]
    a["M_wkb"] = np.zeros((P, H, 2, 32), np.float32)
    a["M_wkb"][0:16, :, 0] = wkvb.reshape(16, H, 32)
    a["M_wkb"] = a["M_wkb"].reshape(P, 8, P)
    a["M_wvb"] = np.zeros((P, 512), np.float32)
    a["M_wvb"][0:16] = wkvb
    a["M_wo"] = tiles(np.ascontiguousarray(i["L1_ffn_Wo"].reshape(H, 64, D)[:, 0:32]).reshape(512, D))
    a["M_w_ln"] = i["L1_ffn_w_ln1"][:, None]
    freqs = 1.0 / np.float32(100000.0) ** (np.arange(0, 32, 2, dtype=np.float32) / np.float32(32))
    ang = np.outer(np.arange(S, dtype=np.float32), freqs.astype(np.float32)).astype(np.float32)
    cos, sin = np.repeat(np.cos(ang).T, 2, 0), np.repeat(np.sin(ang).T, 2, 0)
    sin[0::2] *= -1.0
    one, nil = np.ones((32, S), np.float32), np.zeros((32, S), np.float32)

    def table(plain, rotated):
        return np.tile(np.concatenate([plain, rotated]), (2, 2))
    root = np.float32(64) ** np.float32(-0.5)
    a["M_rope_q"] = np.stack([table(one, cos), table(nil, sin)], 1).astype(np.float32) * root
    a["M_rope_k"] = np.stack([table(nil, cos), table(nil, sin)], 1).astype(np.float32)
    a["M_bias"] = tiles(np.where(pos[:, None] >= pos[None, :], np.float32(0), np.float32(-1e30)))
    a["order"] = np.tile(16.0 - np.arange(16, dtype=np.float32), (P, 1))
    return a


def kernel(**inputs):
    import numpy as np
    import concourse.bacc as bacc
    from concourse.bass_utils import run_bass_kernel_spmd

    arrays = lay_out({k: np.asarray(v) for k, v in inputs.items()})
    nc = bacc.Bacc("TRN2", target_bir_lowering=False, num_devices=1)
    a = {k: nc.dram_tensor(f"in_{k}", v.shape, mybir.dt.from_np(v.dtype), kind="ExternalInput").ap()
         for k, v in arrays.items()}
    out = nc.dram_tensor("out", (P, NT, D), F32, kind="ExternalOutput").ap()
    build(nc, a, out)
    r = run_bass_kernel_spmd(nc, [{f"in_{k}": v for k, v in arrays.items()}], core_ids=[0])
    return r.results[0]["out"].swapaxes(0, 1).reshape(B, S, D)
```
